# Optimizing a Trainium2 kernel written in Bass

```python
import numpy as np
import jax
import jax.numpy as jnp

def _softmax(x, axis=-1):
    return jax.nn.softmax(x, axis=axis)

def _gelu(x):
    return jax.nn.gelu(x, approximate=True)

def _silu(x):
    return jax.nn.silu(x)

def _sigmoid(x):
    return jax.nn.sigmoid(x)

def _layernorm(x, axis=-1, eps=1e-05):
    m = jnp.mean(x, axis=axis, keepdims=True)
    v = jnp.var(x, axis=axis, keepdims=True)
    return (x - m) / jnp.sqrt(v + eps)

def _scatter_add(tgt, idx, src, axis=0):
    return tgt.at[idx].add(src)

def _segment_sum(src, seg, n):
    return jax.ops.segment_sum(src, seg, n)
kernel_name = 'mk_seq_preln_d2_jaxref_r8_f60ef3'

def setup_inputs(seed: int=0):
    np.random.seed(seed)
    _w = jnp.asarray

    def _L0_attn_setup():
        import jax, jax.numpy as jnp
        import numpy as np
        B, S, D, H = (2, 256, 128, 16)
        MASK_VAL = -50000.0
        key = jax.random.key(seed)
        k1, k2, k3, k4 = jax.random.split(key, 4)
        s = 1.0 / np.sqrt(D)
        return {'x': jax.random.normal(k1, (B, S, D), dtype=jnp.float32), 'Wq': jax.random.normal(k2, (D, D), dtype=jnp.float32) * s, 'Wkv': jax.random.normal(k3, (D, 2 * D), dtype=jnp.float32) * s, 'Wo': jax.random.normal(k4, (D, D), dtype=jnp.float32) * s}
    _L0_attn_in = _L0_attn_setup()

    def _L0_ffn_setup():
        import jax, jax.numpy as jnp
        import numpy as np
        B, S, D, H, E = (8, 256, 128, 512, 16)
        key = jax.random.key(seed)
        ks = jax.random.split(key, 4)
        sd = 1.0 / np.sqrt(D).astype(np.float32)
        sh = 1.0 / np.sqrt(H).astype(np.float32)
        return {'x': jax.random.normal(ks[0], (B, S, D), jnp.float32), 'Wg': jax.random.normal(ks[1], (D, E), jnp.float32) * sd, 'bg': jnp.zeros((E,), jnp.float32), 'W1': jax.random.normal(ks[2], (E, D, H), jnp.float32) * sd, 'b1': jnp.zeros((E, H), jnp.float32), 'W2': jax.random.normal(ks[3], (E, H, D), jnp.float32) * sh, 'b2': jnp.zeros((E, D), jnp.float32)}
    _L0_ffn_in = _L0_ffn_setup()

    def _L1_attn_setup():
        import jax, jax.numpy as jnp
        import numpy as np
        import math
        B, L, D_MODEL = (8, 256, 128)
        D_INNER, D_SSM = (256, 128)
        KEY_DIM, VALUE_DIM, H = (96, 192, 4)
        DK, DV = (KEY_DIM // H, VALUE_DIM // H)
        D_CONV = 4
        EPS = 1e-05

        def _dwconv(x, w, b):
            y = jax.lax.conv_general_dilated(x, w, window_strides=(1,), padding=[(1, 2)], dimension_numbers=('NCH', 'OIH', 'NCH'), feature_group_count=x.shape[1])
            return y + b[None, :, None]

        def _l2norm(x):
            return x * jax.lax.rsqrt(jnp.sum(x * x, axis=-1, keepdims=True) + 1e-06)

        def _gated_delta_rule(q, k, v, beta, gk):
            qT = jnp.moveaxis(q, 2, 0)
            kT = jnp.moveaxis(k, 2, 0)
            vT = jnp.moveaxis(v, 2, 0)
            bT = jnp.moveaxis(beta, 2, 0)
            gT = jnp.moveaxis(gk, 2, 0)
            S0 = jnp.zeros((q.shape[0], q.shape[1], q.shape[3], v.shape[3]), q.dtype)

            def step(S, inp):
                qt, kt, vt, bt, gt = inp
                S = S * jnp.exp(gt)[..., None, None]
                u = bt[..., None] * (vt - jnp.einsum('bhk,bhkv->bhv', kt, S))
                S = S + jnp.einsum('bhk,bhv->bhkv', kt, u)
                ot = jnp.einsum('bhk,bhkv->bhv', qt, S)
                return (S, ot)
            _, o = jax.lax.scan(step, S0, (qT, kT, vT, bT, gT))
            return jnp.moveaxis(o, 0, 2)
        key = jax.random.key(seed)
        ks = jax.random.split(key, 20)

        def w(k, shape, fan_in):
            return jax.random.normal(k, shape, jnp.float32) / np.sqrt(fan_in)
        dt = jnp.exp(jax.random.uniform(ks[14], (H,)) * (math.log(0.1) - math.log(0.001)) + math.log(0.001))
        dt = jnp.clip(dt, 0.0001)
        dt_bias = dt + jnp.log(-jnp.expm1(-dt))
        A = jax.random.uniform(ks[13], (H,), minval=0.5, maxval=16.0)
        return {'x': jax.random.normal(ks[0], (B, L, D_MODEL), jnp.float32), 'W_in': w(ks[1], (D_MODEL, D_INNER), D_MODEL), 'conv_x_w': w(ks[2], (D_SSM, 1, D_CONV), D_CONV), 'conv_x_b': jnp.zeros((D_SSM,), jnp.float32), 'conv_z_w': w(ks[3], (D_SSM, 1, D_CONV), D_CONV), 'conv_z_b': jnp.zeros((D_SSM,), jnp.float32), 'W_q': w(ks[4], (D_SSM, KEY_DIM), D_SSM), 'W_k': w(ks[5], (D_SSM, KEY_DIM), D_SSM), 'W_v': w(ks[6], (D_SSM, VALUE_DIM), D_SSM), 'W_g': w(ks[7], (D_SSM, VALUE_DIM), D_SSM), 'W_gk': w(ks[8], (D_SSM, H), D_SSM), 'W_b': w(ks[9], (D_SSM, H), D_SSM), 'b_b': jnp.zeros((H,), jnp.float32), 'A_log': jnp.log(A), 'dt_bias': dt_bias, 'g_norm_w': jnp.ones((DV,), jnp.float32), 'W_so': w(ks[10], (VALUE_DIM, D_SSM), VALUE_DIM), 'W_out': w(ks[11], (D_INNER, D_MODEL), D_INNER)}
    _L1_attn_in = _L1_attn_setup()

    def _L1_ffn_setup():
        import jax, jax.numpy as jnp
        import numpy as np
        DIM = 128

        def _reference_tuple_inner(x, W_r, W_k, W_v, mu_r, mu_k):
            B, T, C = x.shape
            x_prev = jnp.concatenate([jnp.zeros((B, 1, C), x.dtype), x[:, :-1, :]], axis=1)
            xr = mu_r * x + (1.0 - mu_r) * x_prev
            xk = mu_k * x + (1.0 - mu_k) * x_prev
            r = jax.nn.sigmoid(jnp.einsum('btc,dc->btd', xr, W_r))
            k = jnp.einsum('btc,dc->btd', xk, W_k)
            k_act = jnp.square(jax.nn.relu(k))
            out = r * jnp.einsum('btc,dc->btd', k_act, W_v)
            new_state = x[:, -1, :]
            return (out, new_state)
        key = jax.random.key(seed)
        ks = jax.random.split(key, 6)
        B, T, C = (8, 256, DIM)
        x = jax.random.normal(ks[0], (B, T, C), dtype=jnp.float32)
        s = 1.0 / np.sqrt(C)
        W_r = jax.random.uniform(ks[1], (C, C), jnp.float32, -s, s)
        W_k = jax.random.uniform(ks[2], (C, C), jnp.float32, -s, s)
        W_v = jax.random.uniform(ks[3], (C, C), jnp.float32, -s, s)
        mu_r = jax.random.uniform(ks[4], (C,), jnp.float32)
        mu_k = jax.random.uniform(ks[5], (C,), jnp.float32)
        return {'x': x, 'W_r': W_r, 'W_k': W_k, 'W_v': W_v, 'mu_r': mu_r, 'mu_k': mu_k}
    _L1_ffn_in = _L1_ffn_setup()
    _d = {'L0_attn_x': _L0_attn_in['x'], 'L0_attn_Wq': _L0_attn_in['Wq'], 'L0_attn_Wkv': _L0_attn_in['Wkv'], 'L0_attn_Wo': _L0_attn_in['Wo'], 'L0_ffn_Wg': _L0_ffn_in['Wg'], 'L0_ffn_bg': _L0_ffn_in['bg'], 'L0_ffn_W1': _L0_ffn_in['W1'], 'L0_ffn_b1': _L0_ffn_in['b1'], 'L0_ffn_W2': _L0_ffn_in['W2'], 'L0_ffn_b2': _L0_ffn_in['b2'], 'L1_attn_W_in': _L1_attn_in['W_in'], 'L1_attn_conv_x_w': _L1_attn_in['conv_x_w'], 'L1_attn_conv_x_b': _L1_attn_in['conv_x_b'], 'L1_attn_conv_z_w': _L1_attn_in['conv_z_w'], 'L1_attn_conv_z_b': _L1_attn_in['conv_z_b'], 'L1_attn_W_q': _L1_attn_in['W_q'], 'L1_attn_W_k': _L1_attn_in['W_k'], 'L1_attn_W_v': _L1_attn_in['W_v'], 'L1_attn_W_g': _L1_attn_in['W_g'], 'L1_attn_W_gk': _L1_attn_in['W_gk'], 'L1_attn_W_b': _L1_attn_in['W_b'], 'L1_attn_b_b': _L1_attn_in['b_b'], 'L1_attn_A_log': _L1_attn_in['A_log'], 'L1_attn_dt_bias': _L1_attn_in['dt_bias'], 'L1_attn_g_norm_w': _L1_attn_in['g_norm_w'], 'L1_attn_W_so': _L1_attn_in['W_so'], 'L1_attn_W_out': _L1_attn_in['W_out'], 'L1_ffn_W_r': _L1_ffn_in['W_r'], 'L1_ffn_W_k': _L1_ffn_in['W_k'], 'L1_ffn_W_v': _L1_ffn_in['W_v'], 'L1_ffn_mu_r': _L1_ffn_in['mu_r'], 'L1_ffn_mu_k': _L1_ffn_in['mu_k']}
    _x0 = _d['L0_attn_x']
    _d['L0_attn_x'] = jax.random.normal(jax.random.fold_in(jax.random.key(seed), 1), (2, 1024, 128), dtype=_x0.dtype)
    del _x0
    return _d

def reference(L0_attn_x, L0_attn_Wq, L0_attn_Wkv, L0_attn_Wo, L0_ffn_Wg, L0_ffn_bg, L0_ffn_W1, L0_ffn_b1, L0_ffn_W2, L0_ffn_b2, L1_attn_W_in, L1_attn_conv_x_w, L1_attn_conv_x_b, L1_attn_conv_z_w, L1_attn_conv_z_b, L1_attn_W_q, L1_attn_W_k, L1_attn_W_v, L1_attn_W_g, L1_attn_W_gk, L1_attn_W_b, L1_attn_b_b, L1_attn_A_log, L1_attn_dt_bias, L1_attn_g_norm_w, L1_attn_W_so, L1_attn_W_out, L1_ffn_W_r, L1_ffn_W_k, L1_ffn_W_v, L1_ffn_mu_r, L1_ffn_mu_k):

    def _L0_attn_ref(x, Wq, Wkv, Wo):
        import jax, jax.numpy as jnp
        import numpy as np
        B, S, D, H = (2, 256, 128, 16)
        MASK_VAL = -50000.0
        b, sl, d = x.shape
        h = H
        hd = d // h
        scale = hd ** (-0.5)
        q = x @ Wq
        kv = x @ Wkv
        k, v = jnp.split(kv, 2, axis=-1)
        q = q.reshape(b, sl, h, hd).transpose(0, 2, 1, 3)
        k = k.reshape(b, sl, h, hd).transpose(0, 2, 1, 3)
        v = v.reshape(b, sl, h, hd).transpose(0, 2, 1, 3)
        dots = jnp.einsum('bhid,bhjd->bhij', q * scale, k)
        causal = jnp.tril(jnp.ones((sl, sl), dtype=bool))
        dots = jnp.where(causal, dots, MASK_VAL)
        attn = jax.nn.softmax(dots, axis=-1)
        out = jnp.einsum('bhij,bhjd->bihd', attn, v).reshape(b, sl, d)
        return out @ Wo

    def _L0_ffn_ref(x, Wg, bg, W1, b1, W2, b2):
        import jax, jax.numpy as jnp
        import numpy as np
        B, S, D, H, E = (8, 256, 128, 512, 16)
        d = x.shape[-1]
        xf = x.reshape(-1, d)
        n_tok = xf.shape[0]
        n_exp = Wg.shape[1]
        cap = -(-n_tok // n_exp)
        score = jax.nn.softmax(xf @ Wg + bg, axis=-1)
        gate = jnp.max(score, axis=-1)
        idx = jnp.argmax(score, axis=-1)
        onehot = jax.nn.one_hot(idx, n_exp, dtype=jnp.int32)
        pos = jnp.sum((jnp.cumsum(onehot, axis=0) - 1) * onehot, axis=-1)
        keep = pos < cap
        safe_pos = jnp.where(keep, pos, cap - 1)
        buf = jnp.zeros((n_exp, cap, d), x.dtype).at[idx, safe_pos].add(jnp.where(keep[:, None], xf, 0.0))
        h = jax.nn.relu(jnp.einsum('ecd,edh->ech', buf, W1) + b1[:, None, :])
        y = jnp.einsum('ech,ehd->ecd', h, W2) + b2[:, None, :]
        out = y[idx, safe_pos] * gate[:, None]
        out = jnp.where(keep[:, None], out, 0.0)
        return out.reshape(x.shape)

    def _L1_attn_ref(x, W_in, conv_x_w, conv_x_b, conv_z_w, conv_z_b, W_q, W_k, W_v, W_g, W_gk, W_b, b_b, A_log, dt_bias, g_norm_w, W_so, W_out):
        import jax, jax.numpy as jnp
        import numpy as np
        import math
        B, L, D_MODEL = (8, 256, 128)
        D_INNER, D_SSM = (256, 128)
        KEY_DIM, VALUE_DIM, H = (96, 192, 4)
        DK, DV = (KEY_DIM // H, VALUE_DIM // H)
        D_CONV = 4
        EPS = 1e-05

        def _dwconv(x, w, b):
            y = jax.lax.conv_general_dilated(x, w, window_strides=(1,), padding=[(1, 2)], dimension_numbers=('NCH', 'OIH', 'NCH'), feature_group_count=x.shape[1])
            return y + b[None, :, None]

        def _l2norm(x):
            return x * jax.lax.rsqrt(jnp.sum(x * x, axis=-1, keepdims=True) + 1e-06)

        def _gated_delta_rule(q, k, v, beta, gk):
            qT = jnp.moveaxis(q, 2, 0)
            kT = jnp.moveaxis(k, 2, 0)
            vT = jnp.moveaxis(v, 2, 0)
            bT = jnp.moveaxis(beta, 2, 0)
            gT = jnp.moveaxis(gk, 2, 0)
            S0 = jnp.zeros((q.shape[0], q.shape[1], q.shape[3], v.shape[3]), q.dtype)

            def step(S, inp):
                qt, kt, vt, bt, gt = inp
                S = S * jnp.exp(gt)[..., None, None]
                u = bt[..., None] * (vt - jnp.einsum('bhk,bhkv->bhv', kt, S))
                S = S + jnp.einsum('bhk,bhv->bhkv', kt, u)
                ot = jnp.einsum('bhk,bhkv->bhv', qt, S)
                return (S, ot)
            _, o = jax.lax.scan(step, S0, (qT, kT, vT, bT, gT))
            return jnp.moveaxis(o, 0, 2)
        b, l, _ = x.shape
        xz = jnp.swapaxes(x @ W_in, 1, 2)
        xc, zc = jnp.split(xz, 2, axis=1)
        xs = jax.nn.silu(_dwconv(xc, conv_x_w, conv_x_b))
        zs = jax.nn.silu(_dwconv(zc, conv_z_w, conv_z_b))
        xs = jnp.swapaxes(xs, 1, 2)
        q = (xs @ W_q).reshape(b, l, H, DK).transpose(0, 2, 1, 3)
        k = (xs @ W_k).reshape(b, l, H, DK).transpose(0, 2, 1, 3)
        v = (xs @ W_v).reshape(b, l, H, DV).transpose(0, 2, 1, 3)
        gk = -jnp.exp(A_log) * jax.nn.softplus(xs @ W_gk + dt_bias)
        gk = jnp.swapaxes(gk, 1, 2)
        beta = jnp.swapaxes(jax.nn.sigmoid(xs @ W_b + b_b), 1, 2)
        q = _l2norm(q)
        k = _l2norm(k)
        o = _gated_delta_rule(q, k, v, beta, gk)
        o = o.transpose(0, 2, 1, 3)
        g = (xs @ W_g).reshape(b, l, H, DV)
        o = o * jax.lax.rsqrt(jnp.mean(o * o, axis=-1, keepdims=True) + EPS) * g_norm_w
        o = o * (g * jax.nn.sigmoid(g))
        o = o.reshape(b, l, VALUE_DIM)
        y = o @ W_so
        y = jnp.concatenate([y, jnp.swapaxes(zs, 1, 2)], axis=-1)
        return y @ W_out

    def _L1_ffn_ref(x, W_r, W_k, W_v, mu_r, mu_k):
        import jax, jax.numpy as jnp
        import numpy as np
        DIM = 128

        def _reference_tuple_inner(x, W_r, W_k, W_v, mu_r, mu_k):
            B, T, C = x.shape
            x_prev = jnp.concatenate([jnp.zeros((B, 1, C), x.dtype), x[:, :-1, :]], axis=1)
            xr = mu_r * x + (1.0 - mu_r) * x_prev
            xk = mu_k * x + (1.0 - mu_k) * x_prev
            r = jax.nn.sigmoid(jnp.einsum('btc,dc->btd', xr, W_r))
            k = jnp.einsum('btc,dc->btd', xk, W_k)
            k_act = jnp.square(jax.nn.relu(k))
            out = r * jnp.einsum('btc,dc->btd', k_act, W_v)
            new_state = x[:, -1, :]
            return (out, new_state)
        return _reference_tuple_inner(x, W_r, W_k, W_v, mu_r, mu_k)[0]
    x = L0_attn_x
    x = x + _L0_attn_ref(_layernorm(x, axis=-1), L0_attn_Wq, L0_attn_Wkv, L0_attn_Wo)
    x = x + _L0_ffn_ref(_layernorm(x, axis=-1), L0_ffn_Wg, L0_ffn_bg, L0_ffn_W1, L0_ffn_b1, L0_ffn_W2, L0_ffn_b2)
    x = x + _L1_attn_ref(_layernorm(x, axis=-1), L1_attn_W_in, L1_attn_conv_x_w, L1_attn_conv_x_b, L1_attn_conv_z_w, L1_attn_conv_z_b, L1_attn_W_q, L1_attn_W_k, L1_attn_W_v, L1_attn_W_g, L1_attn_W_gk, L1_attn_W_b, L1_attn_b_b, L1_attn_A_log, L1_attn_dt_bias, L1_attn_g_norm_w, L1_attn_W_so, L1_attn_W_out)
    x = x + _L1_ffn_ref(_layernorm(x, axis=-1), L1_ffn_W_r, L1_ffn_W_k, L1_ffn_W_v, L1_ffn_mu_r, L1_ffn_mu_k)
    return x

_drawn_inputs = setup_inputs


def setup_inputs(seed=0):
    import zlib

    import numpy as np

    out = dict(_drawn_inputs(seed))
    spreads = {'L0_ffn_bg': (0.0, 0.1),
     'L0_ffn_b1': (0.0, 0.423),
     'L0_ffn_b2': (0.0, 0.295),
     'L1_attn_conv_x_b': (0.0, 0.1),
     'L1_attn_conv_z_b': (0.0, 0.1),
     'L1_attn_b_b': (0.0, 2.0),
     'L1_attn_g_norm_w': (1.0, 0.2)}
    factors = {'L1_ffn_W_r': 3.43, 'L1_ffn_mu_r': 6.885}
    for name, (base, spread) in spreads.items():
        noise = np.random.default_rng([zlib.crc32(name.encode()), seed]).standard_normal(out[name].shape)
        drawn = base * np.exp(spread * noise) if base else spread * noise
        out[name] = jnp.asarray(drawn.astype(out[name].dtype))
    for name, factor in factors.items():
        out[name] = (out[name] * factor).astype(out[name].dtype)
    return out
```

```python
from contextlib import ExitStack

import concourse.bass as bass
from concourse import mybir

F32 = mybir.dt.float32
BF16 = mybir.dt.bfloat16
I32 = mybir.dt.int32
U32 = mybir.dt.uint32
ALU = mybir.AluOpType
ACT = mybir.ActivationFunctionType
AX = mybir.AxisListType

P = 128
B, S, D = 2, 1024, 128
NT = B * S
NB = NT // P
BPB = S // P
EPS = 1e-5

H, HD = 16, 8
HG = 4
GR = H // HG
NU = B * GR
SCALE = HD ** -0.5
NPART = 3
Q_TERM = [0, 0, 0, 1, 1, 2]
K_TERM = [0, 1, 2, 0, 1, 0]
NTERM = len(Q_TERM)
KROWS = NTERM * HD
KROWS_M = KROWS + NPART
MASK_VAL = -50000.0

E, FF = 16, 512
CAP = -(-NT // E)
FC = FF // P
WSLOT = 4

CH = 32
NC = S // CH
GH, DK, DV = 4, 24, 48


def score_tiles():
    for a in range(HG // 2):
        for qb in range(BPB):
            n = (qb + 1) * P
            for k0 in range(0, n, 512):
                for j in range(2):
                    yield a, j, qb, k0, min(512, n - k0)


def prob_tiles():
    for c in range(S // 512):
        for kb in range(4 * c + 4):
            q0 = max(kb * P, c * 512)
            yield c, kb, q0, (c + 1) * 512 - q0


STILES = list(score_tiles())
PTILES = list(prob_tiles())
NS = len(STILES)
NPT = len(PTILES)
LEAD = 1536
C0T = 4


def score_schedule():
    counts, done, cols, want = [], 0, 0, LEAD
    for n in range(2 * NPT + 1):
        while done < NS and (cols < want or n == 2 * NPT):
            cols += STILES[done][4]
            done += 1
        counts.append(done)
        if n < 2 * NPT:
            want += 2 * PTILES[n // 2][3]
    return counts


SENT = score_schedule()


class Count:

    def __init__(self, eng, sem):
        self.eng, self.sem, self.n = eng, sem, 0

    def fence(self, ins):
        self.n += 1
        ins.then_inc(self.sem, 1)
        self.eng.wait_ge(self.sem, self.n)


def program(nc, t):
    ctx = ExitStack()
    with ctx:
        def sb(name, shape, dt, stack=ctx):
            return stack.enter_context(nc.sbuf_tensor(name, shape, dt))

        def sem(name):
            return ctx.enter_context(nc.semaphore(name))

        ps = ctx.enter_context(nc.psum_tensor("ps", [P, 8, 512], F32))

        def bank(i):
            return ps[:, i, :]

        X = sb("X", [P, NB, D], F32)
        XN = sb("XN", [P, NB, D], F32)
        XT = sb("XT", [P, NT], F32)
        bst = sb("bst", [P, NB, 6], F32)
        mv = sb("mv", [P, NB, 2], F32)
        ve = sb("ve", [P, NB], F32)
        rstd = sb("rstd", [P, NB], F32)
        neghalf = sb("neghalf", [P, 2 * NB * B], F32)
        ident = sb("ident", [P, P], F32)
        identb = sb("identb", [P, P], BF16)
        ones = sb("ones", [P, P], F32)

        x_tok = t["L0_attn_x"].rearrange("b (k p) d -> p (b k) d", p=P)
        out_tok = t["out"].rearrange("b (k p) d -> p (b k) d", p=P)

        ld_x = [sem(f"ld_x{i}") for i in range(4)]
        ld_w = sem("ld_w")
        cst = sem("cst")
        ln_var = sem("ln_var")
        ln_rstd = sem("ln_rstd")
        ln_xn = sem("ln_xn")
        ln_tr = sem("ln_tr")
        ln_xt = sem("ln_xt")
        s_dve, s_act, s_pool = sem("s_dve"), sem("s_act"), sem("s_pool")
        s_out = sem("s_out")

        def ln_stats(v, q):
            for j in range(4 * q, 4 * q + 4):
                i = nc.vector.bn_stats(bst[:, j, :], X[:, j, :])
            v.fence(i)
            for j in range(4 * q, 4 * q + 4):
                i = nc.vector.bn_aggr(mv[:, j, :], bst[:, j, :])
            v.fence(i)
            nc.vector.tensor_scalar(ve[:, 4 * q:4 * q + 4], mv[:, 4 * q:4 * q + 4, 1], EPS, None,
                                    ALU.add).then_inc(ln_var, 1)

        def ln_power(pool, k, q):
            pool.wait_ge(ln_var, 4 * k + q + 1)
            nc.gpsimd.tensor_tensor(rstd[:, 4 * q:4 * q + 4], ve[:, 4 * q:4 * q + 4],
                                    neghalf[:, 0:4], ALU.pow).then_inc(ln_rstd, 1)

        def ln_apply(dve, k, q):
            dve.wait_ge(ln_rstd, 4 * k + q + 1)
            if k and q == 0:
                dve.wait_ge(ln_tr, 4 * k)
            for j in range(4 * q, 4 * q + 4):
                i = nc.vector.tensor_scalar(XN[:, j, :], X[:, j, :], mv[:, j, 0:1], rstd[:, j:j + 1],
                                            ALU.subtract, ALU.mult)
            i.then_inc(ln_xn, 1)

        def ln_transpose(pe, k, q, b):
            pe.wait_ge(ln_xn, 4 * k + q + 1)
            for j in range(4):
                i = nc.tensor.transpose(bank(b)[:, j * P:(j + 1) * P], XN[:, 4 * q + j, :], ident[:, :])
            i.then_inc(ln_tr, 1)

        def ln_copy(act, k, q, b):
            act.wait_ge(ln_tr, 4 * k + q + 1)
            nc.scalar.activation(XT[:, 512 * q:512 * q + 512], bank(b), ACT.Copy).then_inc(ln_xt, 1)

        W1s = sb("W1s", [P, WSLOT, FF], F32)
        W2s = sb("W2s", [P, WSLOT, FC, D], F32)
        Wg = sb("Wg", [P, E], F32)
        bgr = sb("bgr", [1, E], F32)
        b2t = sb("b2t", [P, E, D], F32)
        b2r = b2t[0:1, :, :]
        b1row = sb("b1row", [E * FC, P], F32)
        zero = sb("zero", [P, D], F32)
        Wn = sb("Wn", [P, 3, D], F32)
        mu = sb("mu", [P, 2], F32)
        om = sb("om", [P, 2], F32)
        d_ld = sem("d_ld")
        places = nc.dram_tensor("places", [2 * NT, D], F32, kind="Internal").ap()
        answers = nc.dram_tensor("answers", [NT, D], F32, kind="Internal").ap()
        b_w = [sem(f"b_w{i}") for i in range(WSLOT)]
        b_cw = sem("b_cw")
        b_zero = sem("b_zero")
        b_fill = sem("b_fill")
        b_y = sem("b_y")

        def expert_weights(sp, e):
            if e >= WSLOT:
                sp.wait_ge(b_y, e - WSLOT + 1)
            s = e % WSLOT
            sp.dma_start(W1s[:, s, :], t["L0_ffn_W1"][e]).then_inc(b_w[s], 16)
            sp.dma_start(W2s[:, s, :, :], t["L0_ffn_W2"][e].rearrange("(c p) d -> p c d", p=P)).then_inc(b_w[s], 16)

        def expert_constants(sp):
            sp.wait_ge(b_zero, 1)
            sp.dma_start(places[0:NT, :].rearrange("(k p) d -> p k d", p=P),
                         zero[:, :].unsqueeze(1).to_broadcast([P, NB, D])).then_inc(b_fill, 16)
            sp.dma_start(Wg[:, :], t["L0_ffn_Wg"]).then_inc(b_cw, 16)
            sp.dma_start(bgr[:, :], t["L0_ffn_bg"].rearrange("(a e) -> a e", a=1)).then_inc(b_cw, 16)
            sp.dma_start(b2r[:, :, :], t["L0_ffn_b2"].rearrange("(a e) d -> a e d", a=1)).then_inc(b_cw, 16)
            sp.dma_start(b1row[:, :], t["L0_ffn_b1"].rearrange("e (c p) -> (e c) p", p=P)).then_inc(b_cw, 16)
            for e in range(WSLOT):
                expert_weights(sp, e)
            for i, name in enumerate(("W_r", "W_k", "W_v")):
                sp.dma_start(Wn[:, i, :], t["L1_ffn_" + name]).then_inc(d_ld, 16)
            for i, name in enumerate(("mu_r", "mu_k")):
                sp.dma_start(mu[:, i:i + 1], t["L1_ffn_" + name].rearrange("(p a) -> p a", a=1)).then_inc(d_ld, 16)

        actx = ExitStack()
        Wq = sb("Wq", [P, D], F32, actx)
        Wkv = sb("Wkv", [P, 2 * D], F32, actx)
        WoP = sb("WoP", [P, GR, D], F32, actx)
        selD = sb("selD", [P, HG], F32, actx)
        maskS = sb("maskS", [P, P], BF16, actx)
        maskT = sb("maskT", [P, P], BF16, actx)
        QP = sb("QP", [P, NPART, NT], BF16, actx)
        KP = sb("KP", [P, NPART, NT], BF16, actx)
        rem = sb("rem", [P, 3, 512], F32, actx)
        V = sb("V", [P, NB, D], F32, actx)
        QS = sb("QS", [P, GR, HG // 2, S], BF16, actx)
        KS = sb("KS", [P, 2, GR, HG // 2, S], BF16, actx)
        VX = sb("VX", [P, 2, BPB, HG, 32], F32, actx)
        PR = sb("PR", [P, 2, HG, 512], F32, actx)
        mx0 = sb("mx0", [P, 2, 2, HG // 2, BPB], F32, actx)
        mx1 = sb("mx1", [P, 2, 2, HG // 2, BPB // 2], F32, actx)
        m3 = sb("m3", [P, 2, 2, NPART, HG // 2 * BPB], BF16, actx)
        mr = sb("mr", [P, 2, 2, HG // 2 * BPB], F32, actx)
        MT = sb("MT", [NPART * HG * BPB, 2, P], BF16, actx)
        OT = sb("OT", [P, GR, S], F32, actx)
        RC = sb("RC", [P, 2, 4 * HG], F32, actx)
        Dq = nc.dram_tensor("Dq", [H, NTERM, HD, NT], BF16, kind="Internal").ap()
        Dk = nc.dram_tensor("Dk", [H, NTERM, HD, NT], BF16, kind="Internal").ap()

        a_wz = sem("a_wz")
        a_pps = sem("a_pps")
        a_hi = sem("a_hi")
        a_rem = sem("a_rem")
        a_mid = sem("a_mid")
        a_part = sem("a_part")
        a_vps = sem("a_vps")
        a_v = sem("a_v")
        a_dq = sem("a_dq")
        a_dk = sem("a_dk")
        a_stk = [sem(f"a_stk{i}") for i in range(GR)]
        a_s = sem("a_s")
        a_mx = sem("a_mx")
        a_m3 = sem("a_m3")
        a_mtp = sem("a_mtp")
        a_mt = sem("a_mt")
        a_mrow = [sem(f"a_mrow{i}") for i in range(2)]
        a_st = sem("a_st")
        a_p = sem("a_p")
        a_pv = sem("a_pv")
        a_vx = sem("a_vx")
        a_ot = sem("a_ot")
        a_bc = sem("a_bc")
        a_rc = sem("a_rc")
        a_sp = sem("a_sp")
        a_on = sem("a_on")
        a_y = sem("a_y")
        a_x = sem("a_x")

        SB = (0, 1)
        PVB, MB = 6, 7

        def loads(sp):
            for i in range(4):
                sp.dma_start(X[:, 4 * i:4 * i + 4, :], x_tok[:, 4 * i:4 * i + 4, :]).then_inc(ld_x[i], 16)
            sp.dma_start(Wq[:, :], t["L0_attn_Wq"]).then_inc(ld_w, 16)
            sp.dma_start(Wkv[:, :], t["L0_attn_Wkv"]).then_inc(ld_w, 16)
            sp.wait_ge(a_wz, 1)
            wo = t["L0_attn_Wo"].rearrange("(g e d) n -> e d g n", g=GR, e=HG)
            for e in range(HG):
                sp.dma_start(WoP[32 * e:32 * e + HD, :, :], wo[e]).then_inc(ld_w, 16)

        def a_sync(sp):
            for b in range(B):
                sp.wait_ge(a_part, 4 * (b + 1))
                cols = slice(b * S, (b + 1) * S)
                for n in range(NTERM):
                    sp.dma_start(Dq[:, n, :, cols], QP[:, Q_TERM[n], cols]).then_inc(a_dq, 16)
                    sp.dma_start(Dk[:, n, :, cols], KP[:, K_TERM[n], cols]).then_inc(a_dk, 16)
                if b == 0:
                    for u in range(GR):
                        stack_loads(sp, u)
                    expert_constants(sp)
            max_rows(sp, 0)
            for u in range(NU):
                if u + 1 < NU:
                    max_rows(sp, u + 1)
                if u + GR < NU:
                    stack_loads(sp, u + GR)

        def stack_loads(sp, u):
            b, g = divmod(u, GR)
            sp.wait_ge(a_dq, 16 * NTERM * (b + 1))
            sp.wait_ge(a_dk, 16 * NTERM * (b + 1))
            if u == 0:
                sp.wait_ge(a_wz, 4)
            if u == GR:
                sp.wait_ge(b_zero, 1)
            if b:
                sp.wait_ge(a_pv, NPT * (u - GR + 1))
            for j in range(2):
                if b:
                    sp.dma_start(QS[64 * j + KROWS:64 * j + KROWS_M, g, :, :],
                                 zero[0:NPART * HG // 2 * S // (2 * D), :].bitcast(BF16)).then_inc(a_stk[g], 16)
                for dst, src in ((QS, Dq), (KS[:, j], Dk)):
                    sp.dma_start(dst[64 * j:64 * j + KROWS, g, :, :],
                                 src[4 * g + j:4 * g + 4:2, :, :, b * S:(b + 1) * S].rearrange("a n d t -> (n d) a t")
                                 ).then_inc(a_stk[g], 16)

        def max_rows(q, u):
            q.wait_ge(a_mt, u + 1)
            half = NPART * HG // 2 * BPB
            for j in range(2):
                q.dma_start(QS[64 * j + KROWS:64 * j + KROWS_M, u % GR, :, :].rearrange("n a (k p) -> n (a k) p", p=P),
                            MT[half * j:half * j + half, u % 2, :]).then_inc(a_mrow[u % 2], 16)

        def a_pool(pool, c):
            nc.gpsimd.memset(WoP[:, :, :], 0.0).then_inc(a_wz, 1)
            c.fence(nc.gpsimd.memset(ident[:, :], 0.0))
            nc.gpsimd.affine_select(out=ident[:, :], in_=ident[:, :], compare_op=ALU.not_equal, fill=1.0,
                                    base=0, pattern=[[-1, P]], channel_multiplier=1).then_inc(cst, 1)
            nc.gpsimd.memset(neghalf[:, :], -0.5).then_inc(cst, 1)
            for q in range(4):
                if q == 0:
                    pool.wait_ge(cst, 2)
                ln_power(pool, 0, q)
            c.fence(nc.gpsimd.memset(identb[:, :], 0.0))
            nc.gpsimd.affine_select(out=identb[:, :], in_=identb[:, :], compare_op=ALU.not_equal, fill=1.0,
                                    base=0, pattern=[[-1, P]], channel_multiplier=1).then_inc(cst, 1)
            pool.wait_ge(cst, 3)
            c.fence(nc.gpsimd.memset(KS[:, :, :, :, :].rearrange("p j g a s -> p (j g a s)").bitcast(F32), 0.0))
            for j in range(2):
                nc.gpsimd.memset(KS[64 * j + 32:64 * j + 64, j, :, :, :], 1.0).then_inc(a_wz, 1)
                pool.wait_ge(a_wz, j + 2)
            nc.gpsimd.memset(QS[:, :, :, :].rearrange("p g a s -> p (g a s)").bitcast(F32), 0.0).then_inc(a_wz, 1)
            nc.gpsimd.memset(ones[:, :], 1.0).then_inc(cst, 1)
            c.fence(nc.gpsimd.memset(maskS[:, :], 0.0))
            nc.gpsimd.affine_select(out=maskS[:, :], in_=maskS[:, :], compare_op=ALU.is_ge, fill=MASK_VAL,
                                    base=0, pattern=[[-1, P]], channel_multiplier=1).then_inc(cst, 1)
            c.fence(nc.gpsimd.memset(maskT[:, :], 0.0))
            nc.gpsimd.affine_select(out=maskT[:, :], in_=maskT[:, :], compare_op=ALU.is_ge, fill=MASK_VAL,
                                    base=0, pattern=[[1, P]], channel_multiplier=-1).then_inc(cst, 1)
            c.fence(nc.gpsimd.memset(selD[:, :], 0.0))
            nc.gpsimd.affine_select(out=selD[:, :], in_=selD[:, :], compare_op=ALU.not_equal, fill=1.0,
                                    base=-HD, pattern=[[-32, HG]], channel_multiplier=1).then_inc(cst, 1)
            nc.gpsimd.memset(zero[:, :], 0.0).then_inc(b_zero, 1)
            c.fence(nc.gpsimd.memset(VX[:, :, :, :, :], 0.0))
            c.fence(nc.gpsimd.memset(VX[:, :, :, :, HD:HD + 1], 1.0))
            for u in range(NU):
                b, g = divmod(u, GR)
                pool.wait_ge(a_v, 2 * (b + 1))
                if u >= 2:
                    pool.wait_ge(a_pv, NPT * (u - 1))
                nc.gpsimd.tensor_copy(
                    VX[:, u % 2, :, :, 0:HD],
                    V[:, b * BPB:(b + 1) * BPB, 32 * g:32 * g + 32].rearrange("p k (e d) -> p k e d", d=HD),
                ).then_inc(a_vx, 1)

        PIECES = [(c, w) for c in range(4) for w in range(2)]

        def a_pe(pe):
            pe.wait_ge(cst, 2)
            for c in range(4):
                ln_transpose(pe, 0, c, MB)
                pe.wait_ge(ln_xt, c + 1)
                if c == 0:
                    pe.wait_ge(ld_w, 96)
                for w in range(2):
                    n = 2 * c + w
                    if n >= 4:
                        pe.wait_ge(a_part, n - 3)
                    lhs = Wq[:, :] if w == 0 else Wkv[:, 0:D]
                    nc.tensor.matmul(bank(n % 4), lhs, XT[:, 512 * c:512 * c + 512],
                                     start=True, stop=True).then_inc(a_pps, 1)
                if c >= 2:
                    pe.wait_ge(a_v, c - 1)
                for j in range(4):
                    i = nc.tensor.matmul(bank(4 + c % 2)[:, j * P:(j + 1) * P],
                                         XT[:, (4 * c + j) * P:(4 * c + j + 1) * P], Wkv[:, D:2 * D],
                                         start=True, stop=True)
                i.then_inc(a_vps, 1)
            pe.wait_ge(cst, 7)
            pe.wait_ge(a_v, 4)
            for i in range(NS):
                score_piece(pe, 0, i)
            transpose_max(pe, 0)
            for u in range(NU):
                next_scores(pe, u + 1, 0)
                pe.wait_ge(a_mrow[u % 2], 32 * (u // 2 + 1))
                pe.wait_ge(a_vx, u + 1)
                for n in range(2 * NPT):
                    prob_piece(pe, u, n)
                    next_scores(pe, u + 1, n + 1)
                    if n % 2 == 0 and n >= 2:
                        times_v(pe, u, n // 2 - 1)
                    if n == 4 and u >= 1:
                        turn_sums(pe, u - 1, 1)
                    if n == 7 and u >= 1:
                        spread_sums(pe, u - 1, 1)
                    if n == 9 and u == GR:
                        project_out(pe, 0)
                    if n == 14:
                        turn_sums(pe, u, 0)
                    if n == 17:
                        spread_sums(pe, u, 0)
                times_v(pe, u, NPT - 1)
                if u + 1 < NU:
                    transpose_max(pe, u + 1)
            turn_sums(pe, NU - 1, 1)
            spread_sums(pe, NU - 1, 1)
            project_out(pe, 1)

        def next_scores(pe, u, n):
            if u < NU:
                for i in range(SENT[n - 1] if n else 0, SENT[n]):
                    score_piece(pe, u, i)

        def score_piece(pe, u, i):
            a, j, qb, k0, n = STILES[i]
            g = u % GR
            if i == 0:
                pe.wait_ge(a_stk[g], 16 * (4 if u < GR else 10))
            m = u * NS + i
            if m >= 2:
                pe.wait_ge(a_mx, m - 1)
            diag = k0 + n == (qb + 1) * P
            o = bank(4 + m % 2)
            mm = nc.tensor.matmul(o[:, 0:n], QS[:, g, a, qb * P:(qb + 1) * P], KS[:, j, g, a, k0:k0 + n],
                                  start=True, stop=not diag)
            if diag:
                mm = nc.tensor.matmul(o[:, n - P:n], identb[:, :], maskS[:, :], start=False, stop=True)
            mm.then_inc(a_s, 1)

        def transpose_max(pe, u):
            pe.wait_ge(a_m3, u + 1)
            if u >= 1:
                pe.wait_ge(a_mt, u)
            if u >= 1:
                pe.wait_ge(a_on, 2 * u - 1)
            nc.tensor.transpose(bank(MB).bitcast(BF16)[0:NPART * HG * BPB, 0:P],
                                m3[:, u % 2, :, :, :].rearrange("p j n k -> p (j n k)"), identb[:, :]).then_inc(a_mtp, 1)

        def prob_piece(pe, u, n):
            c, kb, q0, w = PTILES[n // 2]
            m = 2 * NPT * u + n
            if m >= 2:
                pe.wait_ge(a_p, m - 1)
            g = u % GR
            diag = q0 == kb * P
            for j in range(2):
                mm = nc.tensor.matmul(bank(2 * (n % 2) + j)[:, 0:w], KS[:, j, g, n % 2, kb * P:(kb + 1) * P],
                                      QS[:, g, n % 2, q0:q0 + w], start=True, stop=not diag)
            for j in range(2):
                if diag:
                    mm = nc.tensor.matmul(bank(2 * (n % 2) + j)[:, 0:P], identb[:, :], maskT[:, :],
                                          start=False, stop=True)
            mm.then_inc(a_st, 1)

        def times_v(pe, u, i):
            c, kb, q0, w = PTILES[i]
            last = 4 * c + 3
            pe.wait_ge(a_p, 2 * NPT * u + 2 * i + 2)
            if kb == 0 and 2 * u + c >= 1:
                pe.wait_ge(a_ot, 2 * u + c)
            for e in range(HG):
                mm = nc.tensor.matmul(bank(PVB)[32 * e:32 * e + 32, q0 - c * 512:512],
                                      VX[:, u % 2, kb, e, :], PR[:, i % 2, e, 0:w],
                                      start=kb == 0, stop=kb == last)
            mm.then_inc(a_pv, 1)

        def turn_sums(pe, u, c):
            n = 2 * u + c
            pe.wait_ge(a_ot, n + 1)
            pe.wait_ge(a_mt, min(u + 1 + c, NU))
            if n >= 1:
                pe.wait_ge(a_on, n)
            if n == 2 * GR:
                pe.wait_ge(a_x, 2)
            for j in range(4):
                q0 = c * 512 + j * P
                mm = nc.tensor.matmul(bank(MB)[:, HG * j:HG * j + HG], OT[:, u % GR, q0:q0 + P], selD[:, :],
                                      start=True, stop=True)
            mm.then_inc(a_bc, 1)

        def spread_sums(pe, u, c):
            n = 2 * u + c
            pe.wait_ge(a_rc, n + 1)
            for j in range(4):
                for e in range(HG):
                    r = RC[:, n % 2, HG * j + e:HG * j + e + 1].to_broadcast([P, 32])
                    mm = nc.tensor.matmul(bank(MB)[32 * e:32 * e + 32, j * P:(j + 1) * P], r, ident[:, :],
                                          start=True, stop=True)
            mm.then_inc(a_sp, 1)

        def project_out(pe, b):
            pe.wait_ge(a_on, 8 * (b + 1))
            for k in range(2):
                if k or b:
                    pe.wait_ge(a_x, 2 * b + k)
                for j in range(4):
                    kb = 4 * k + j
                    for g in range(GR):
                        mm = nc.tensor.matmul(bank(MB)[:, j * P:(j + 1) * P], OT[:, g, kb * P:(kb + 1) * P],
                                              WoP[:, g, :], start=g == 0, stop=g == GR - 1)
                mm.then_inc(a_y, 1)

        def a_act(act):
            for n in range(len(PIECES) + 1):
                if n % 2 == 0 and n < 8:
                    ln_copy(act, 0, n // 2, MB)
                if n < len(PIECES):
                    part_hi(act, n)
                if n >= 1:
                    part_mid(act, n - 1)
                if n % 2 == 1:
                    q = n // 2
                    act.wait_ge(a_vps, q + 1)
                    nc.scalar.activation(V[:, 4 * q:4 * q + 4, :].rearrange("p k d -> p (k d)"),
                                         bank(4 + q % 2), ACT.Copy).then_inc(a_v, 1)
            copy_max(act, 0)
            for u in range(NU):
                for n in range(2 * NPT):
                    m = 2 * NPT * u + n
                    i = n // 2
                    c, kb, q0, w = PTILES[i]
                    if kb == 1 and n % 2 == 0 and c == 1:
                        copy_out(act, u, 0)
                    if kb == 1 and n % 2 == 0 and c == 0 and u >= 1:
                        copy_out(act, u - 1, 1)
                    act.wait_ge(a_st, m + 1)
                    if NPT * u + i >= 2:
                        act.wait_ge(a_pv, NPT * u + i - 1)
                    nc.scalar.activation(PR[:, i % 2, 2 * (n % 2):2 * (n % 2) + 2, 0:w],
                                         ps[:, 2 * (n % 2):2 * (n % 2) + 2, 0:w], ACT.Exp).then_inc(a_p, 1)
                if u + 1 < NU:
                    copy_max(act, u + 1)
            copy_out(act, NU - 1, 1)

        def dst_parts(n):
            c, w = PIECES[n]
            return (QP if w == 0 else KP), slice(512 * c, 512 * c + 512), (SCALE if w == 0 else 1.0)

        def part_hi(act, n):
            dst, cols, s = dst_parts(n)
            act.wait_ge(a_pps, n + 1)
            nc.scalar.activation(dst[:, 0, cols], bank(n % 4), ACT.Copy, scale=s).then_inc(a_hi, 1)

        def part_mid(act, n):
            dst, cols, s = dst_parts(n)
            act.wait_ge(a_rem, n + 1)
            nc.scalar.activation(dst[:, 1, cols], rem[:, n % 3, :], ACT.Copy).then_inc(a_mid, 1)

        def copy_max(act, u):
            act.wait_ge(a_mtp, u + 1)
            if u >= 2:
                act.wait_ge(a_mrow[u % 2], 32 * (u // 2))
            nc.scalar.activation(MT[:, u % 2, :], bank(MB).bitcast(BF16)[0:NPART * HG * BPB, 0:P],
                                 ACT.Copy).then_inc(a_mt, 1)

        def copy_out(act, u, c):
            act.wait_ge(a_pv, NPT * u + (C0T if c == 0 else NPT))
            if u == GR:
                act.wait_ge(a_y, 2)
            nc.scalar.activation(OT[:, u % GR, c * 512:c * 512 + 512], bank(PVB), ACT.Copy).then_inc(a_ot, 1)

        def a_dve(dve, v):
            for q in range(4):
                dve.wait_ge(ld_x[q], 16)
                ln_stats(v, q)
            for n in range(len(PIECES) + 1):
                if n % 2 == 0 and n < 8:
                    ln_apply(dve, 0, n // 2)
                if n < len(PIECES):
                    dst, cols, s = dst_parts(n)
                    dve.wait_ge(a_hi, n + 1)
                    if n >= 3:
                        dve.wait_ge(a_part, n - 2)
                    nc.vector.scalar_tensor_tensor(rem[:, n % 3, :], bank(n % 4), s, dst[:, 0, cols],
                                                   ALU.mult, ALU.subtract).then_inc(a_rem, 1)
                if n >= 1:
                    dst, cols, s = dst_parts(n - 1)
                    dve.wait_ge(a_mid, n)
                    nc.vector.tensor_tensor(dst[:, 2, cols], rem[:, (n - 1) % 3, :], dst[:, 1, cols],
                                            ALU.subtract).then_inc(a_part, 1)
            for u in range(NU):
                for i in range(NS):
                    reduce_piece(dve, u, i)
                    if i == SENT[5] - 1 and u >= 2:
                        reciprocal(dve, u - 2, 1)
                    if i == SENT[8] - 1 and u >= 2:
                        normalise(dve, u - 2, 1)
                    if i == SENT[10] - 1 and u == GR + 1:
                        residual(dve, 0)
                    if i == SENT[15] - 1 and u >= 1:
                        reciprocal(dve, u - 1, 0)
                    if i == SENT[18] - 1 and u >= 1:
                        normalise(dve, u - 1, 0)
                unit_max(dve, v, u)
            for u, c in ((NU - 2, 1), (NU - 1, 0), (NU - 1, 1)):
                reciprocal(dve, u, c)
                normalise(dve, u, c)
            residual(dve, 1)

        def reduce_piece(dve, u, i):
            a, j, qb, k0, n = STILES[i]
            m = u * NS + i
            if i == 0 and u >= 2:
                dve.wait_ge(a_mtp, u - 1)
            dve.wait_ge(a_s, m + 1)
            o = mx0[:, u % 2, j, a, qb:qb + 1] if k0 == 0 else mx1[:, u % 2, j, a, qb - 4:qb - 3]
            nc.vector.tensor_reduce(o, bank(4 + m % 2)[:, 0:n], AX.X, ALU.max).then_inc(a_mx, 1)

        def unit_max(dve, v, u):
            r = u % 2
            dve.wait_ge(a_mx, NS * (u + 1))
            v.fence(nc.vector.tensor_tensor(mx0[:, r, :, :, 4:8], mx0[:, r, :, :, 4:8], mx1[:, r, :, :, :], ALU.max))
            m = mx0[:, r, :, :, :].rearrange("p j a k -> p j (a k)")
            v.fence(nc.vector.tensor_scalar(m3[:, r, :, 0, :], m, -1.0, None, ALU.mult))
            v.fence(nc.vector.scalar_tensor_tensor(mr[:, r, :, :], m, -1.0, m3[:, r, :, 0, :], ALU.mult, ALU.subtract))
            v.fence(nc.vector.tensor_copy(m3[:, r, :, 1, :], mr[:, r, :, :]))
            nc.vector.tensor_tensor(m3[:, r, :, 2, :], mr[:, r, :, :], m3[:, r, :, 1, :], ALU.subtract).then_inc(a_m3, 1)

        def reciprocal(dve, u, c):
            n = 2 * u + c
            dve.wait_ge(a_bc, n + 1)
            nc.vector.reciprocal(RC[:, n % 2, :], bank(MB)[:, 0:4 * HG]).then_inc(a_rc, 1)

        def normalise(dve, u, c):
            n = 2 * u + c
            dve.wait_ge(a_sp, n + 1)
            o = OT[:, u % GR, c * 512:c * 512 + 512]
            nc.vector.tensor_tensor(o, bank(MB), o, ALU.mult).then_inc(a_on, 1)

        def residual(dve, b):
            for k in range(2):
                dve.wait_ge(a_y, 2 * b + k + 1)
                x = X[:, 8 * b + 4 * k:8 * b + 4 * k + 4, :].rearrange("p k d -> p (k d)")
                nc.vector.tensor_tensor(x, bank(MB), x, ALU.add).then_inc(a_x, 1)

        actx.close()

        cctx = ExitStack()
        NH = NC // 2 * B
        KTx = sb("KTx", [P, NH, P], F32, cctx)
        QGx = sb("QGx", [P, NH, P], F32, cctx)
        ATx = sb("ATx", [P, NH, P], F32, cctx)
        KDx = sb("KDx", [P, NH, P], F32, cctx)
        W2x = sb("W2x", [P, NH, P], F32, cctx)
        c_z = sem("c_z")

        bctx = ExitStack()
        trib = sb("trib", [P, P], BF16, bctx)
        oneb = sb("oneb", [P, P], BF16, bctx)
        iotae = sb("iotae", [P, NB, E], F32, bctx)
        itok = sb("itok", [P, NB], F32, bctx)
        first = sb("first", [P, E, NB], F32, bctx)
        lg = sb("lg", [P, NB, E], F32, bctx)
        lmax = sb("lmax", [P, NB], F32, bctx)
        lexp = sb("lexp", [P, NB, E], F32, bctx)
        lsum = sb("lsum", [P, NB], F32, bctx)
        gate = sb("gate", [P, NB], F32, bctx)
        cand = sb("cand", [P, NB, E], F32, bctx)
        cmin = sb("cmin", [P, NB], F32, bctx)
        oh = sb("oh", [P, NB, E], BF16, bctx)
        tot = sb("tot", [P, E, NB], F32, bctx)
        run = sb("run", [P, E, NB], F32, bctx)
        pose = sb("pose", [P, NB, E], F32, bctx)
        pos = sb("pos", [P, NB], F32, bctx)
        keep = sb("keep", [P, NB], F32, bctx)
        base = sb("base", [P, NB], F32, bctx)
        tmp = sb("tmp", [P, 2, NB], F32, bctx)
        sidx = sb("sidx", [P, NB], U32, bctx)
        gidx = sb("gidx", [P, NB], U32, bctx)
        b1T = sb("b1T", [P, E * FC], F32, bctx)
        BT = sb("BT", [P, E, D], F32, bctx)
        BTT = sb("BTT", [P, 2, P], F32, bctx)
        hs = sb("hs", [P, 2, FC, P], F32, bctx)
        YS = sb("YS", [P, E, D], F32, bctx)
        G = sb("G", [P, NB, D], F32, bctx)

        b_cst = sem("b_cst")
        b_lg = sem("b_lg")
        b_d = sem("b_d")
        b_e = sem("b_e")
        b_oh = sem("b_oh")
        b_cnt = sem("b_cnt")
        b_idx = sem("b_idx")
        b_sc = sem("b_sc")
        b_ld = [sem(f"b_ld{i}") for i in range(4)]
        b_b1 = sem("b_b1")
        b_t = sem("b_t")
        b_tt = sem("b_tt")
        b_h = sem("b_h")
        b_rv = sem("b_rv")
        b_ra = sem("b_ra")
        b_ys = sem("b_ys")
        b_ans = sem("b_ans")
        b_g = [sem(f"b_g{i}") for i in range(4)]
        b_x = sem("b_x")

        def b_sync(sp):
            for i in range(4):
                if i == 0:
                    sp.wait_ge(b_sc, 16 * NB)
                sp.dma_start(BT[:, 4 * i:4 * i + 4, :],
                             places[512 * i:512 * i + 512, :].rearrange("(e p) d -> p e d", p=P)
                             ).then_inc(b_ld[i], 16)
            for e in range(E):
                if e >= WSLOT:
                    expert_weights(sp, e)
                if e % 4 == 3 and e >= 2 * WSLOT - 1:
                    answers_out(sp, e // 4 - 1)
            answers_out(sp, 3)

        def answers_out(sp, i):
            sp.wait_ge(b_ys, 4 * i + 4)
            sp.dma_start(answers[512 * i:512 * i + 512, :].rearrange("(e p) d -> p e d", p=P),
                         YS[:, 4 * i:4 * i + 4, :]).then_inc(b_ans, 16)

        def b_pool(pool, c):
            pool.wait_ge(a_x, 4)
            c.fence(nc.gpsimd.memset(trib[:, :], 1.0))
            nc.gpsimd.affine_select(out=trib[:, :], in_=trib[:, :], compare_op=ALU.is_gt, fill=0.0,
                                    base=0, pattern=[[1, P]], channel_multiplier=-1).then_inc(b_cst, 1)
            nc.gpsimd.memset(oneb[:, :], 1.0).then_inc(b_cst, 1)
            nc.gpsimd.iota(iotae[:, :, :], pattern=[[0, NB], [1, E]], base=0, channel_multiplier=0,
                           allow_small_or_imprecise_dtypes=True).then_inc(b_cst, 1)
            nc.gpsimd.iota(itok[:, :], pattern=[[P, NB]], base=NT, channel_multiplier=1,
                           allow_small_or_imprecise_dtypes=True).then_inc(b_cst, 1)
            c.fence(nc.gpsimd.memset(first[:, :, :], 1.0))
            nc.gpsimd.memset(first[:, :, 0:1], 0.0).then_inc(b_cst, 1)
            for q in range(4):
                ln_power(pool, 1, q)
            pool.wait_ge(b_idx, 1)
            pool.wait_ge(b_fill, 16)
            for j in range(NB):
                nc.gpsimd.indirect_dma_start(
                    out=places[:, :], out_offset=bass.IndirectOffsetOnAxis(ap=sidx[:, j:j + 1], axis=0),
                    in_=XN[:, j, :], in_offset=None).then_inc(b_sc, 16)
            for x in (KTx, QGx, ATx, KDx, W2x):
                nc.gpsimd.memset(x[:, :, :], 0.0).then_inc(c_z, 1)
            pool.wait_ge(b_ans, 64)
            for j in range(NB):
                nc.gpsimd.indirect_dma_start(
                    out=G[:, j, :], out_offset=None, in_=answers[:, :],
                    in_offset=bass.IndirectOffsetOnAxis(ap=gidx[:, j:j + 1], axis=0)).then_inc(b_g[j // 4], 16)

        def b_pe(pe):
            pe.wait_ge(b_cw, 64)
            for q in range(4):
                ln_transpose(pe, 1, q, (0, 1, 5, 6)[q])
            nc.tensor.transpose(bank(7)[:, 0:E * FC], b1row[:, :], ident[0:E * FC, 0:E * FC]).then_inc(b_b1, 1)
            for j in range(NB):
                if j % 4 == 0:
                    pe.wait_ge(ln_xt, 4 + j // 4 + 1)
                o = bank(2)[:, j * E:(j + 1) * E]
                nc.tensor.matmul(o, XT[:, j * P:(j + 1) * P], Wg[:, :], start=True, stop=False)
                mm = nc.tensor.matmul(o, ones[0:1, :], bgr[:, :], start=False, stop=True)
            mm.then_inc(b_lg, 1)
            pe.wait_ge(b_oh, 1)
            pe.wait_ge(b_cst, 2)
            ohf = oh[:, :, :].rearrange("p k e -> p (k e)")
            nc.tensor.matmul(bank(3)[:, 0:NB * E], trib[:, :], ohf, start=True, stop=True)
            nc.tensor.matmul(bank(4)[:, 0:NB * E], oneb[:, :], ohf, start=True, stop=True).then_inc(b_cnt, 1)
            expert_turn(pe, 0)
            for e in range(E):
                if e + 1 < E:
                    expert_turn(pe, e + 1)
                pe.wait_ge(b_tt, e + 1)
                pe.wait_ge(b_w[e % WSLOT], 32 * (e // WSLOT + 1))
                if e >= 2:
                    pe.wait_ge(b_ra, e - 1)
                    pe.wait_ge(b_rv, e - 1)
                else:
                    pe.wait_ge(b_idx, 1)
                    pe.wait_ge(b_b1, 2)
                for f in range(FC):
                    mm = nc.tensor.matmul(hidden(e, f),
                                          W1s[:, e % WSLOT, f * P:(f + 1) * P], BTT[:, e % 2, :],
                                          start=True, stop=True)
                mm.then_inc(b_h, 1)
                if e >= 1:
                    expert_answer(pe, e - 1)
            expert_answer(pe, E - 1)

        def hidden(e, f):
            return bank((2, 6)[e % 2] + f // 2)[:, f % 2 * P:(f % 2 + 1) * P]

        def expert_turn(pe, e):
            pe.wait_ge(b_ld[e // 4], 16)
            if e >= 2:
                pe.wait_ge(b_tt, e - 1)
            elif e == 0:
                pe.wait_ge(ln_xt, 8)
            nc.tensor.transpose(bank(e % 2)[:, 0:P], BT[:, e, :], ident[:, :]).then_inc(b_t, 1)

        def expert_answer(pe, e):
            pe.wait_ge(b_ra, e + 1)
            pe.wait_ge(b_rv, e + 1)
            if e >= 2:
                pe.wait_ge(b_ys, e - 1)
            o = bank(4 + e % 2)[:, 0:D]
            for f in range(FC):
                nc.tensor.matmul(o, hs[:, e % 2, f, :], W2s[:, e % WSLOT, f, :], start=f == 0, stop=False)
            nc.tensor.matmul(o, ones[0:1, :], b2r[:, e, :], start=False, stop=True).then_inc(b_y, 1)

        def b_act(act):
            for q in range(4):
                if q == 0:
                    act.wait_ge(a_y, 4)
                ln_copy(act, 1, q, (0, 1, 5, 6)[q])
            act.wait_ge(b_b1, 1)
            nc.scalar.activation(b1T[:, :], bank(7)[:, 0:E * FC], ACT.Copy).then_inc(b_b1, 1)
            act.wait_ge(b_d, 1)
            nc.scalar.activation(lexp[:, :, :], lg[:, :, :], ACT.Exp).then_inc(b_e, 1)
            act.wait_ge(b_b1, 2)
            expert_copy(act, 0)
            for e in range(E):
                if e + 1 < E:
                    expert_copy(act, e + 1)
                act.wait_ge(b_h, e + 1)
                if e >= 2:
                    act.wait_ge(b_y, e - 1)
                for f in (2, 3):
                    i = nc.scalar.activation(hs[:, e % 2, f, :], hidden(e, f), ACT.Relu,
                                             bias=b1T[:, e * FC + f:e * FC + f + 1])
                i.then_inc(b_ra, 1)
                if e >= 1:
                    answer_copy(act, e - 1)
            answer_copy(act, E - 1)

        def expert_copy(act, e):
            act.wait_ge(b_t, e + 1)
            if e >= 2:
                act.wait_ge(b_h, e - 1)
            nc.scalar.activation(BTT[:, e % 2, :], bank(e % 2)[:, 0:P], ACT.Copy).then_inc(b_tt, 1)

        def answer_copy(act, e):
            act.wait_ge(b_y, e + 1)
            nc.scalar.activation(YS[:, e, :], bank(4 + e % 2)[:, 0:D], ACT.Copy).then_inc(b_ys, 1)

        def b_dve(dve, v):
            dve.wait_ge(a_x, 4)
            for q in range(4):
                ln_stats(v, q)
            for q in range(4):
                ln_apply(dve, 1, q)
            dve.wait_ge(b_lg, 1)
            dve.wait_ge(b_cst, 5)
            p3 = bank(2)[:, 0:NB * E].rearrange("p (k e) -> p k e", e=E)

            def over(x):
                return x.unsqueeze(2).to_broadcast([P, NB, E])

            v.fence(nc.vector.tensor_reduce(lmax[:, :], p3, AX.X, ALU.max))
            v.fence(nc.vector.tensor_tensor(lg[:, :, :], p3, over(lmax[:, :]), ALU.subtract))
            i = nc.vector.tensor_scalar(cand[:, :, :], lg[:, :, :], 0.0, -float(E), ALU.is_ge, ALU.mult)
            i.then_inc(b_d, 1)
            dve.wait_ge(b_d, 1)
            v.fence(nc.vector.tensor_tensor(cand[:, :, :], cand[:, :, :], iotae[:, :, :], ALU.add))
            v.fence(nc.vector.tensor_reduce(cmin[:, :], cand[:, :, :], AX.X, ALU.min))
            nc.vector.tensor_tensor(oh[:, :, :], cand[:, :, :], over(cmin[:, :]), ALU.is_equal).then_inc(b_oh, 1)
            dve.wait_ge(b_e, 1)
            v.fence(nc.vector.tensor_reduce(lsum[:, :], lexp[:, :, :], AX.X, ALU.add))
            nc.vector.reciprocal(gate[:, :], lsum[:, :])
            v.fence(nc.vector.tensor_scalar(base[:, :], cmin[:, :], float(E), float(CAP), ALU.add, ALU.mult))
            dve.wait_ge(b_cnt, 1)
            v.fence(nc.vector.tensor_copy(tot[:, :, :], bank(4)[:, 0:NB * E].rearrange("p (k e) -> p e k", e=E)))
            v.fence(nc.vector.tensor_tensor_scan(
                run[:, :, :].rearrange("p e k -> p (e k)"), first[:, :, :].rearrange("p e k -> p (e k)"),
                tot[:, :, :].rearrange("p e k -> p (e k)"), 0.0, ALU.mult, ALU.add))
            v.fence(nc.vector.tensor_tensor(run[:, :, :], run[:, :, :], tot[:, :, :], ALU.subtract))
            v.fence(nc.vector.tensor_tensor(pose[:, :, :], bank(3)[:, 0:NB * E].rearrange("p (k e) -> p k e", e=E),
                                            run[:, :, :].rearrange("p e k -> p k e"), ALU.add))
            v.fence(nc.vector.tensor_tensor(pose[:, :, :], pose[:, :, :], oh[:, :, :], ALU.mult))
            v.fence(nc.vector.tensor_reduce(pos[:, :], pose[:, :, :], AX.X, ALU.add))
            nc.vector.tensor_scalar(keep[:, :], pos[:, :], float(CAP), None, ALU.is_lt)
            nc.vector.tensor_tensor(tmp[:, 0, :], base[:, :], pos[:, :], ALU.add)
            v.fence(nc.vector.tensor_scalar(tmp[:, 1, :], pos[:, :], float(CAP - 1), None, ALU.min))
            nc.vector.tensor_tensor(gidx[:, :], base[:, :], tmp[:, 1, :], ALU.add)
            nc.vector.tensor_tensor(gate[:, :], gate[:, :], keep[:, :], ALU.mult)
            v.fence(nc.vector.tensor_tensor(tmp[:, 0, :], tmp[:, 0, :], itok[:, :], ALU.subtract))
            v.fence(nc.vector.tensor_tensor(tmp[:, 0, :], tmp[:, 0, :], keep[:, :], ALU.mult))
            nc.vector.tensor_tensor(sidx[:, :], tmp[:, 0, :], itok[:, :], ALU.add).then_inc(b_idx, 1)
            dve.wait_ge(b_b1, 2)
            for e in range(E):
                dve.wait_ge(b_h, e + 1)
                if e >= 2:
                    dve.wait_ge(b_y, e - 1)
                for f in (0, 1):
                    i = nc.vector.tensor_scalar(hs[:, e % 2, f, :], hidden(e, f),
                                                b1T[:, e * FC + f:e * FC + f + 1], 0.0, ALU.add, ALU.max)
                i.then_inc(b_rv, 1)
            for j in range(NB):
                if j % 4 == 0:
                    dve.wait_ge(b_g[j // 4], 64)
                nc.vector.scalar_tensor_tensor(X[:, j, :], G[:, j, :], gate[:, j:j + 1], X[:, j, :],
                                               ALU.mult, ALU.add).then_inc(b_x, 1)

        bctx.close()

        HT = S // 2
        HC = NC // 2
        NPJ = 2 * DK + 2 * DV + 2
        PJG = 3
        NG = -(-NH // PJG)
        RW = DV + 32
        RG = 512 // RW
        NR = -(-NH // RG)
        LP_ = 1
        KQ = W1s[:, :, :].rearrange("p a b -> p (a b)").rearrange("p (n c) -> p n c", c=64)
        XS = W2s[:, :, :, :].rearrange("p a b c -> p (a b c)")
        ZS = XN[:, :, :].rearrange("p k d -> p (k d)")
        KN = XT[:, 0:NH * 32].rearrange("p (n k) -> p n k", k=32)
        QN = XT[:, NH * 32:2 * NH * 32].rearrange("p (n k) -> p n k", k=32)
        XC = sb("XC", [P, B, S + 3], F32, cctx)
        ZC = sb("ZC", [P, B, S + 3], F32, cctx)
        PJ = sb("PJ", [P, NH, NPJ], F32, cctx)
        Ed = XC[:, 0, 0:S].rearrange("p (n s) -> p n s", s=32)
        Et = XC[:, 1, 0:S].rearrange("p (n s) -> p n s", s=32)
        Lp = sb("Lp", [P, 32, 32], F32, cctx)
        Mp = sb("Mp", [P, 32, 32], F32, cctx)
        mt = sb("mt", [P, 256], F32, cctx)
        R = sb("R", [P, NH, RW], F32, cctx)
        Wd = sb("Wd", [P, NH, RW], F32, cctx)
        Lc = Wd[:, :, 0:32]
        Os = b2t[:, :, :].rearrange("p e d -> p (e d)").rearrange("p (n v) -> p n v", v=64)
        YT = ZC[:, :, 0:HT]
        Sx = sb("Sx", [P, B, 2, DV], F32, cctx)
        Win = sb("Win", [P, 2 * D], F32, cctx)
        WC = sb("WC", [P, GH, NPJ], F32, cctx)
        wgb = sb("wgb", [P, 2, GH], F32, cctx)
        WS = sb("WS", [P, 2, D], F32, cctx)
        Wou = sb("Wou", [P, 2, D], F32, cctx)
        cw = sb("cw", [P, 2, 4], F32, cctx)
        cb = sb("cb", [P, 2], F32, cctx)
        gn = sb("gn", [P, DV], F32, cctx)
        par = sb("par", [P, 3], F32, cctx)
        dgw = sb("dgw", [P, 4, P], F32, cctx)
        tri = sb("tri", [P, P], F32, cctx)
        blk = sb("blk", [P, P], F32, cctx)
        dmask = sb("dmask", [P, 32], F32, cctx)
        sm = sb("sm", [P, 16, NH], F32, cctx)
        OT0, OT1 = Ed, Et
        gsum = mt[:, 0:3 * NH].rearrange("p (a n) -> p a n", a=3)
        ss = mt[:, 3 * NH:5 * NH].rearrange("p (n a) -> p n a", a=2)
        rs = mt[:, 5 * NH:7 * NH].rearrange("p (n a) -> p n a", a=2)

        c_ld = sem("c_ld")
        c_wz = sem("c_wz")
        c_cst = sem("c_cst")
        c_xc = sem("c_xc")
        c_xce = sem("c_xce")
        c_pad = sem("c_pad")
        c_wc = sem("c_wc")
        c_dg = sem("c_dg")
        c_cv = sem("c_cv")
        c_xs = sem("c_xs")
        c_zp = sem("c_zp")
        c_zs = sem("c_zs")
        c_pj = sem("c_pj")
        c_pje = sem("c_pje")
        c_ss = sem("c_ss")
        c_rs = sem("c_rs")
        c_n = sem("c_n")
        c_kq = sem("c_kq")
        c_kx = sem("c_kx")
        c_gr = sem("c_gr")
        c_zz = sem("c_zz")
        c_ga = sem("c_ga")
        c_gk = sem("c_gk")
        c_gc = sem("c_gc")
        c_gs = sem("c_gs")
        c_ge = sem("c_ge")
        c_be = sem("c_be")
        c_dd = sem("c_dd")
        c_ed = sem("c_ed")
        c_r = sem("c_r")
        c_kd = sem("c_kd")
        c_qg = sem("c_qg")
        c_qx = sem("c_qx")
        c_at = sem("c_at")
        c_mi = sem("c_mi")
        c_tt = sem("c_tt")
        c_w = sem("c_w")
        c_we = sem("c_we")
        c_w2 = sem("c_w2")
        c_clr = sem("c_clr")
        c_x = [sem(f"c_x{b}") for b in range(B)]
        c_u = [sem(f"c_u{b}") for b in range(B)]
        c_sp = [sem(f"c_sp{b}") for b in range(B)]
        c_s = [sem(f"c_s{b}") for b in range(B)]
        c_o = [sem(f"c_o{b}") for b in range(B)]
        c_oe = sem("c_oe")
        c_gg = sem("c_gg")
        c_gw = sem("c_gw")
        c_os = sem("c_os")
        c_or = sem("c_or")
        c_ot = sem("c_ot")
        c_y = sem("c_y")
        c_ye = sem("c_ye")
        c_f = sem("c_f")
        c_fx = sem("c_fx")

        def band(h):
            return slice(32 * h, 32 * h + 32)

        def half_cols(b, hf):
            return slice(b * S + hf * HT, b * S + hf * HT + HT)

        def rowwise(x, w):
            return x.unsqueeze(2).to_broadcast([x.shape[0], NH, w])

        def c_loads(sp):
            sp.wait_ge(b_x, NB)
            sp.wait_ge(c_wz, 1)
            T = lambda n: t["L1_attn_" + n]
            jobs = [(Win[:, :], T("W_in"))]
            at = 0
            for name, w in (("W_q", DK), ("W_k", DK), ("W_v", DV), ("W_g", DV)):
                jobs.append((WC[:, :, at:at + w], T(name).rearrange("p (h k) -> p h k", h=GH)))
                at += w
            jobs += [(wgb[:, 0, :], T("W_gk")), (wgb[:, 1, :], T("W_b"))]
            wso = T("W_so")
            for h in range(GH):
                jobs.append((WS[32 * h:32 * h + 32, 0, :], wso[DV * h:DV * h + 32, :]))
                jobs.append((WS[32 * h:32 * h + DV - 32, 1, :], wso[DV * h + 32:DV * h + DV, :]))
                for i, name in enumerate(("A_log", "dt_bias", "b_b")):
                    jobs.append((par[band(h), i:i + 1],
                                 T(name)[h:h + 1].rearrange("(a b) -> a b", a=1).to_broadcast([32, 1])))
            jobs.append((Wou[:, :, :], T("W_out").rearrange("(a p) n -> p a n", p=P)))
            for i, name in enumerate(("x", "z")):
                jobs.append((cw[:, i, :], T(f"conv_{name}_w").rearrange("p a j -> p (a j)")))
                jobs.append((cb[:, i:i + 1], T(f"conv_{name}_b").rearrange("(p a) -> p a", a=1)))
            jobs.append((gn[:, :], T("g_norm_w").rearrange("(a v) -> a v", a=1).to_broadcast([P, DV])))
            for dst, src in jobs:
                sp.dma_start(dst, src).then_inc(c_ld, 16)
        C_LD = 16 * (1 + 6 + 5 * GH + 1 + 4 + 1)

        def c_pool(pool, c):
            pool.wait_ge(b_x, NB)
            pool.wait_ge(c_z, 5)
            nc.gpsimd.memset(WS[:, :, :], 0.0).then_inc(c_wz, 1)
            for q in range(4):
                ln_power(pool, 2, q)
            for x in (XC, ZC):
                nc.gpsimd.memset(x[:, :, 0:1], 0.0).then_inc(c_pad, 1)
                nc.gpsimd.memset(x[:, :, S + 1:S + 3], 0.0).then_inc(c_pad, 1)
            nc.gpsimd.memset(tri[:, :], 1.0)
            c.fence(nc.gpsimd.memset(blk[:, :], 1.0))
            b4 = lambda x: x[:, :].rearrange("p (h r) -> p h r", h=GH)
            c.fence(nc.gpsimd.affine_select(out=b4(blk), in_=b4(blk), compare_op=ALU.is_ge, fill=0.0, base=0,
                                            pattern=[[-32, GH], [0, 32]], channel_multiplier=1))
            nc.gpsimd.affine_select(out=b4(blk), in_=b4(blk), compare_op=ALU.is_ge, fill=0.0, base=31,
                                    pattern=[[32, GH], [0, 32]], channel_multiplier=-1).then_inc(c_cst, 1)
            c.fence(nc.gpsimd.affine_select(out=tri[:, :], in_=tri[:, :], compare_op=ALU.is_ge, fill=0.0, base=0,
                                            pattern=[[1, P]], channel_multiplier=-1))
            nc.gpsimd.affine_select(out=b4(tri), in_=b4(tri), compare_op=ALU.is_ge, fill=0.0, base=0,
                                    pattern=[[-32, GH], [0, 32]], channel_multiplier=1).then_inc(c_cst, 1)
            c.fence(nc.gpsimd.memset(dmask[:, :], 0.0))
            for h in range(GH):
                c.fence(nc.gpsimd.affine_select(out=dmask[band(h), :], in_=dmask[band(h), :], compare_op=ALU.is_ge,
                                                fill=-1e30, base=0, pattern=[[-1, 32]], channel_multiplier=1))
            c.fence(nc.gpsimd.memset(Os[:, :, DV:64], 0.0))
            c.fence(nc.gpsimd.memset(R[:, :, DV + DK:RW], 0.0))
            nc.gpsimd.memset(Sx[:, :, :, :], 0.0).then_inc(c_clr, 1)
            for hf in range(2):
                if hf == 0:
                    pool.wait_ge(c_xce, 8)
                    nc.gpsimd.memset(KN[:, :, DK:32], 0.0).then_inc(c_clr, 1)
                    nc.gpsimd.memset(QN[:, :, DK:32], 0.0).then_inc(c_clr, 1)
                pool.wait_ge(c_ss, hf + 1)
                nc.gpsimd.tensor_tensor(rs[:, :, :].rearrange("p n a -> p (n a)"),
                                        ss[:, :, :].rearrange("p n a -> p (n a)"),
                                        neghalf[:, 0:2 * NH], ALU.pow).then_inc(c_rs, 1)
                if hf:
                    pool.wait_ge(c_tt, 1)
                c.fence(nc.gpsimd.memset(Mp[:, :, :], 0.0))
                nc.gpsimd.memset(Mp[:, :, :].rearrange("p t s -> p (t s)")[:, 0:32 * 32:33], 1.0).then_inc(c_mi, 1)
                pool.wait_ge(c_n, hf + 1)
                pool.wait_ge(c_ge, hf + 1)
                pool.wait_ge(c_be, hf + 1)
                if hf:
                    for b in range(B):
                        pool.wait_ge(c_o[b], HC)
                    pool.wait_ge(c_os, 1)
                pool.wait_ge(c_kq, hf + 1)
                nc.gpsimd.tensor_tensor(QN[:, :, 0:DK], QN[:, :, 0:DK], rowwise(sm[:, 5, :], DK), ALU.mult
                                        ).then_inc(c_qg, 1)
                nc.gpsimd.tensor_tensor(R[:, :, 0:DV], PJ[:, :, 2 * DK:2 * DK + DV], rowwise(sm[:, 8, :], DV),
                                        ALU.mult).then_inc(c_r, 1)
                nc.gpsimd.tensor_tensor(R[:, :, DV:DV + DK], KN[:, :, 0:DK], rowwise(sm[:, 9, :], DK),
                                        ALU.mult).then_inc(c_r, 1)
                pool.wait_ge(c_r, 2 * hf + 2)
                for h in range(GH):
                    i = nc.gpsimd.tensor_tensor(KDx[band(h), :, 32 * h:32 * h + DK], KN[band(h), :, 0:DK],
                                                rowwise(sm[band(h), 6, :], DK), ALU.mult)
                    i.then_inc(c_kd, 1)
                    pool.wait_ge(c_kd, GH * hf + h + 1)
                pool.wait_ge(c_gg, hf + 1)
                nc.gpsimd.tensor_tensor(PJ[:, :, 2 * DK + DV:2 * DK + 2 * DV], PJ[:, :, 2 * DK + DV:2 * DK + 2 * DV],
                                        gn[:, :].unsqueeze(1).to_broadcast([P, NH, DV]), ALU.mult).then_inc(c_gw, 1)
                pool.wait_ge(c_os, hf + 1)
                nc.gpsimd.tensor_tensor(sm[:, 12, :], sm[:, 11, :], neghalf[:, 0:NH], ALU.pow).then_inc(c_or, 1)

        def c_pe(pe):
            for q in range(4):
                ln_transpose(pe, 2, q, (0, 1, 2, 3)[q])
            pe.wait_ge(c_ld, C_LD)
            pe.wait_ge(b_ys, E)
            for q in range(4):
                pe.wait_ge(ln_xt, 8 + q + 1)
                for w in range(2):
                    n = 2 * q + w
                    if n >= 4:
                        pe.wait_ge(c_xce, n - 3)
                    nc.tensor.matmul(bank(4 + n % 4), Win[:, w * D:(w + 1) * D], XT[:, 512 * q:512 * q + 512],
                                     start=True, stop=True).then_inc(c_xc, 1)
            for hf in range(2):
                pe.wait_ge(c_xs, 2)
                pe.wait_ge(c_wc, 1)
                for g in range(NG):
                    m = hf * NG + g
                    if m >= 2:
                        pe.wait_ge(c_pje, m - 1)
                    if hf == 1 and g == 0:
                        pe.wait_ge(c_oe, 4)
                    for i in range(min(PJG, NH - PJG * g)):
                        n = PJG * g + i
                        b, c = divmod(n, HC)
                        c0 = b * S + hf * HT + CH * c
                        for h in range(GH):
                            mm = nc.tensor.matmul(bank(m % 2)[band(h), i * NPJ:(i + 1) * NPJ], XS[:, c0:c0 + CH],
                                                  WC[:, h, :], start=True, stop=True)
                    mm.then_inc(c_pj, 1)
                pe.wait_ge(c_gk, hf + 1)
                pe.wait_ge(c_cst, 2)
                if hf == 1:
                    pe.wait_ge(c_oe, 4)
                nc.tensor.matmul(bank(6)[:, 0:NH], tri[:, :], sm[:, 2, :], start=True, stop=True)
                nc.tensor.matmul(bank(6)[:, NH:2 * NH], blk[:, :], sm[:, 2, :], start=True, stop=True).then_inc(c_gc, 1)
                pe.wait_ge(c_kx, 4 * hf + 4)
                if hf == 1:
                    pe.wait_ge(c_fx, 2)
                    pe.wait_ge(c_ye, 2)
                for n in range(NH):
                    mm = nc.tensor.matmul(bank(2 + n // 8)[:, n % 8 * 64:(n % 8 + 1) * 64], KTx[:, n, :], KQ[:, n, :],
                                          start=True, stop=True)
                mm.then_inc(c_gr, 1)
                if hf == 0:
                    pe.wait_ge(c_dg, 1)
                    pe.wait_ge(c_xce, 8)
                    pe.wait_ge(c_gs, 1)
                    for q in range(4):
                        b, o = divmod(512 * q, S)
                        if q >= 1:
                            pe.wait_ge(c_zs, q)
                        for j in range(4):
                            mm = nc.tensor.matmul(bank(7), dgw[:, j, :], ZC[:, b, o + j:o + j + 512],
                                                  start=j == 0, stop=j == 3)
                        mm.then_inc(c_zp, 1)
                pe.wait_ge(c_tt, hf + 1)
                pe.wait_ge(c_r, 2 * hf + 2)
                for g in range(NR):
                    m = hf * NR + g
                    if g == 0:
                        pe.wait_ge(c_pje, NG * (hf + 1))
                    if m >= 2:
                        pe.wait_ge(c_we, m - 1)
                    for i in range(min(RG, NH - RG * g)):
                        n = RG * g + i
                        mm = nc.tensor.matmul(bank(g % 2)[:, i * RW:(i + 1) * RW], KTx[:, n, :], R[:, n, :],
                                              start=True, stop=True)
                    mm.then_inc(c_w, 1)
                pe.wait_ge(c_w2, hf + 1)
                pe.wait_ge(c_kd, GH * (hf + 1))
                pe.wait_ge(c_qx, hf + 1)
                pe.wait_ge(c_clr, 1)
                pe.wait_ge(c_we, NR * (hf + 1))
                pe.wait_ge(c_zs, 4)
                pe.wait_ge(c_at, hf + 1)
                for c in range(HC):
                    k = hf * HC + c
                    for b in range(B):
                        if k:
                            pe.wait_ge(c_s[b], k)
                        nc.tensor.matmul(bank(2 + b)[:, 0:DV], W2x[:, b * HC + c, :], Sx[:, b, k % 2, :],
                                         start=True, stop=True).then_inc(c_x[b], 1)
                    for b in range(B):
                        n = b * HC + c
                        pe.wait_ge(c_u[b], k + 1)
                        nc.tensor.matmul(bank(4 + b)[:, 0:DV], KDx[:, n, :], Wd[:, n, 0:DV],
                                         start=True, stop=True).then_inc(c_sp[b], 1)
                        o = bank((6 if c < 8 else 0) + b)[:, c % 8 * DV:(c % 8 + 1) * DV]
                        nc.tensor.matmul(o, QGx[:, n, :], Sx[:, b, k % 2, :], start=True, stop=False)
                        nc.tensor.matmul(o, ATx[:, n, :], Wd[:, n, 0:DV], start=False, stop=True).then_inc(c_o[b], 1)
                pe.wait_ge(c_ot, hf + 1)
                for b in range(B):
                    pe.wait_ge(c_s[b], HC * (hf + 1))
                    pe.wait_ge(c_oe, 4 * hf + 4)
                    for j, x in enumerate((OT0, OT1)):
                        mm = nc.tensor.matmul(bank(2 + b), WS[:, j, :],
                                              x[:, b * HC:(b + 1) * HC, :].rearrange("p n t -> p (n t)"),
                                              start=j == 0, stop=j == 1)
                    mm.then_inc(c_y, 1)
                for b in range(B):
                    pe.wait_ge(c_ye, 2 * hf + b + 1)
                    for j in range(4):
                        o = bank(4 + b)[:, j * P:(j + 1) * P]
                        c0 = b * S + hf * HT + j * P
                        nc.tensor.matmul(o, YT[:, b, j * P:(j + 1) * P], Wou[:, 0, :], start=True, stop=False)
                        mm = nc.tensor.matmul(o, ZS[:, c0:c0 + P], Wou[:, 1, :], start=False, stop=True)
                    mm.then_inc(c_f, 1)

        def c_act(act, ca):
            act.wait_ge(c_ld, C_LD)
            for q in range(4):
                if q == 0:
                    act.wait_ge(b_lg, 1)
                ln_copy(act, 2, q, (0, 1, 2, 3)[q])
            for n in range(8):
                q, w = divmod(n, 2)
                b, o = divmod(512 * q, S)
                act.wait_ge(c_xc, n + 1)
                nc.scalar.activation((XC, ZC)[w][:, b, 1 + o:1 + o + 512], bank(4 + n % 4), ACT.Copy).then_inc(c_xce, 1)
            for b in range(B):
                act.wait_ge(c_cv, b + 1)
                nc.scalar.activation(XS[:, b * S:(b + 1) * S], XS[:, b * S:(b + 1) * S], ACT.Silu).then_inc(c_xs, 1)
            for hf in range(2):
                if hf:
                    act.wait_ge(c_gw, 1)
                for g in range(NG):
                    m = hf * NG + g
                    w = min(PJG, NH - PJG * g)
                    act.wait_ge(c_pj, m + 1)
                    if hf and g == 0:
                        act.wait_ge(c_ot, 1)
                    nc.scalar.activation(PJ[:, PJG * g:PJG * g + w, :].rearrange("p n c -> p (n c)"),
                                         bank(m % 2)[:, 0:w * NPJ], ACT.Copy).then_inc(c_pje, 1)
                act.wait_ge(c_zz, hf + 1)
                ca.fence(nc.scalar.activation(sm[:, 3, :], sm[:, 0, :], ACT.Abs))
                ca.fence(nc.scalar.activation(sm[:, 3, :], sm[:, 3, :], ACT.Exp, scale=-1.0))
                nc.scalar.activation(sm[:, 4, :], sm[:, 3, :], ACT.Ln, bias=1.0)
                nc.scalar.activation(sm[:, 10, :], sm[:, 1, :], ACT.Exp, scale=-1.0)
                nc.scalar.activation(sm[:, 13, 0:1], par[:, 0:1], ACT.Exp).then_inc(c_ga, 1)
                act.wait_ge(c_kq, hf + 1)
                if hf == 0:
                    act.wait_ge(c_z, 5)
                else:
                    act.wait_ge(c_w, NR)
                for h in range(GH):
                    nc.scalar.activation(KTx[band(h), :, 32 * h:32 * h + 32], KQ[band(h), :, 0:32],
                                         ACT.Copy).then_inc(c_kx, 1)
                act.wait_ge(c_gs, hf + 1)
                nc.scalar.activation(sm[:, 5:8, :], gsum[:, :, :], ACT.Exp
                                     ).then_inc(c_ge, 1)
                act.wait_ge(c_dd, hf + 1)
                nc.scalar.activation(Ed[:, :, :], Ed[:, :, :], ACT.Exp).then_inc(c_ed, 1)
                act.wait_ge(c_pje, NG * (hf + 1))
                g0 = 2 * DK + DV
                nc.scalar.activation(PJ[:, :, g0:g0 + DV], PJ[:, :, g0:g0 + DV], ACT.Silu).then_inc(c_gg, 1)
                if hf == 0:
                    for q in range(4):
                        act.wait_ge(c_zp, q + 1)
                        nc.scalar.activation(ZS[:, 512 * q:512 * q + 512], bank(7), ACT.Silu,
                                             bias=cb[:, 1:2]).then_inc(c_zs, 1)
                for g in range(NR):
                    m = hf * NR + g
                    w = min(RG, NH - RG * g)
                    act.wait_ge(c_w, m + 1)
                    nc.scalar.activation(Wd[:, RG * g:RG * g + w, :].rearrange("p n c -> p (n c)"),
                                         bank(g % 2)[:, 0:w * RW], ACT.Copy).then_inc(c_we, 1)
                for g in range(2):
                    for b in range(B):
                        act.wait_ge(c_o[b], hf * HC + 8 * g + 8)
                        n = b * HC + 8 * g
                        nc.scalar.activation(Os[:, n:n + 8, 0:DV],
                                             bank((6 if g == 0 else 0) + b)[:, 0:8 * DV].rearrange(
                                                 "p (n v) -> p n v", v=DV), ACT.Copy).then_inc(c_oe, 1)
                for b in range(B):
                    act.wait_ge(c_y, 2 * hf + b + 1)
                    if hf:
                        act.wait_ge(c_f, b + 1)
                    nc.scalar.activation(YT[:, b, :], bank(2 + b), ACT.Copy).then_inc(c_ye, 1)

        def c_dve(dve, v):
            dve.wait_ge(b_x, NB)
            for q in range(4):
                ln_stats(v, q)
            for q in range(4):
                ln_apply(dve, 2, q)
            dve.wait_ge(c_ld, C_LD)
            nc.vector.tensor_copy(WC[:, :, NPJ - 2:NPJ], wgb[:, :, :].rearrange("p w h -> p h w")).then_inc(c_wc, 1)
            for j in range(4):
                i = nc.vector.tensor_scalar(dgw[:, j, :], ident[:, :], cw[:, 1, j:j + 1], None, ALU.mult)
            i.then_inc(c_dg, 1)
            dve.wait_ge(c_pad, 4)
            for b in range(B):
                dve.wait_ge(c_xce, 4 * b + 3)
                y = XS[:, b * S:(b + 1) * S]
                v.fence(nc.vector.tensor_scalar(y, XC[:, b, 0:S], cw[:, 0, 0:1], cb[:, 0:1], ALU.mult, ALU.add))
                for j in range(1, 4):
                    i = nc.vector.scalar_tensor_tensor(y, XC[:, b, j:j + S], cw[:, 0, j:j + 1], y, ALU.mult, ALU.add)
                    if j < 3:
                        v.fence(i)
                i.then_inc(c_cv, 1)
            for hf in range(2):
                dve.wait_ge(c_pje, NG * (hf + 1))
                if hf:
                    dve.wait_ge(c_or, 1)
                nc.vector.tensor_scalar(sm[:, 0, :], PJ[:, :, NPJ - 2], par[:, 1:2], None, ALU.add)
                nc.vector.tensor_scalar(sm[:, 1, :], PJ[:, :, NPJ - 1], par[:, 2:3], None, ALU.add).then_inc(c_zz, 1)
                if hf:
                    dve.wait_ge(c_w, NR)
                sq = R[:, :, 0:2 * DK]
                v.fence(nc.vector.tensor_tensor(sq, PJ[:, :, 0:2 * DK], PJ[:, :, 0:2 * DK], ALU.mult))
                v.fence(nc.vector.tensor_reduce(ss[:, :, :], sq.rearrange("p n (a k) -> p n a k", k=DK), AX.X, ALU.add))
                nc.vector.tensor_scalar(ss[:, :, :], ss[:, :, :], 1e-6, None, ALU.add).then_inc(c_ss, 1)
                dve.wait_ge(c_ga, hf + 1)
                v.fence(nc.vector.tensor_scalar(sm[:, 14, :], sm[:, 0, :], 0.0, None, ALU.max))
                v.fence(nc.vector.tensor_tensor(sm[:, 14, :], sm[:, 14, :], sm[:, 4, :], ALU.add))
                nc.vector.tensor_scalar(sm[:, 2, :], sm[:, 14, :], sm[:, 13, 0:1], -1.0, ALU.mult, ALU.mult
                                        ).then_inc(c_gk, 1)
                v.fence(nc.vector.tensor_scalar(sm[:, 15, :], sm[:, 10, :], 1.0, None, ALU.add))
                v.fence(nc.vector.reciprocal(sm[:, 8, :], sm[:, 15, :]))
                dve.wait_ge(c_rs, hf + 1)
                if hf == 0:
                    dve.wait_ge(c_clr, 3)
                nc.vector.tensor_tensor(KN[:, :, 0:DK], PJ[:, :, DK:2 * DK], rowwise(rs[:, :, 1], DK), ALU.mult)
                v.fence(nc.vector.tensor_tensor(QN[:, :, 0:DK], PJ[:, :, 0:DK], rowwise(rs[:, :, 0], DK), ALU.mult))
                nc.vector.transpose(KQ[:, :, 0:32], KN[:, :, :]).then_inc(c_n, 1)
                nc.vector.transpose(KQ[:, :, 32:64], QN[:, :, :]).then_inc(c_kq, 1)
                dve.wait_ge(c_gc, hf + 1)
                v.fence(nc.vector.tensor_copy(gsum[:, 0:3:2, :], bank(6)[:, 0:2 * NH].rearrange("p (a n) -> p a n", a=2)))
                nc.vector.tensor_tensor(gsum[:, 1, :], gsum[:, 2, :], gsum[:, 0, :], ALU.subtract).then_inc(c_gs, 1)
                v.fence(nc.vector.transpose(Et[:, :, :], rowwise(gsum[:, 0, :], 32)))
                v.fence(nc.vector.tensor_tensor(Ed[:, :, :], rowwise(gsum[:, 0, :], 32), Et[:, :, :], ALU.subtract))
                nc.vector.tensor_tensor(Ed[:, :, :], Ed[:, :, :], dmask[:, :].unsqueeze(1).to_broadcast([P, NH, 32]),
                                        ALU.add).then_inc(c_dd, 1)
                dve.wait_ge(c_ge, hf + 1)
                nc.vector.tensor_tensor(sm[:, 9, :], sm[:, 8, :], sm[:, 5, :], ALU.mult).then_inc(c_be, 1)
                dve.wait_ge(c_ed, hf + 1)
                v.fence(nc.vector.transpose(Et[:, :, :], Ed[:, :, :]))
                dve.wait_ge(c_gr, hf + 1)
                gram = ps[:, 2:6, :].rearrange("p b (n c) -> p (b n) c", c=64)
                v.fence(nc.vector.tensor_tensor(Lc[:, :, :], gram[:, :, 0:32], Ed[:, :, :], ALU.mult))
                v.fence(nc.vector.scalar_tensor_tensor(Lc[:, :, :], Lc[:, :, :], -1.0, rowwise(sm[:, 8, :], 32),
                                                       ALU.mult, ALU.mult))
                v.fence(nc.vector.transpose(Lp[:, :, :], Lc[:, :, :].rearrange("p n s -> p s n")))
                for h in range(GH):
                    i = nc.vector.tensor_tensor(ATx[band(h), :, 32 * h:32 * h + 32], gram[band(h), :, 32:64],
                                                Et[band(h), :, :], ALU.mult)
                i.then_inc(c_at, 1)
                dve.wait_ge(c_mi, hf + 1)
                for s in range(CH - 1):
                    r, w = CH - 1 - s, s + 1
                    m = mt[:, 0:r * w].rearrange("p (t j) -> p t j", j=w)
                    v.fence(nc.vector.tensor_tensor(m, Lp[:, s, s + 1:CH].unsqueeze(2).to_broadcast([P, r, w]),
                                                    Mp[:, s, 0:w].unsqueeze(1).to_broadcast([P, r, w]), ALU.mult))
                    v.fence(nc.vector.tensor_tensor(Mp[:, s + 1:CH, 0:w], Mp[:, s + 1:CH, 0:w], m, ALU.add))
                for h in range(GH):
                    i = nc.vector.transpose(KTx[band(h), :, 32 * h:32 * h + 32].rearrange("p n t -> p t n"),
                                            Mp[band(h), :, :])
                i.then_inc(c_tt, 1)
                dve.wait_ge(c_qg, hf + 1)
                for h in range(GH):
                    i = nc.vector.transpose(QGx[band(h), :, 32 * h:32 * h + 32], QN[band(h), :, :])
                i.then_inc(c_qx, 1)
                dve.wait_ge(c_we, NR * (hf + 1))
                for h in range(GH):
                    i = nc.vector.transpose(W2x[band(h), :, 32 * h:32 * h + 32], Wd[band(h), :, DV:RW])
                i.then_inc(c_w2, 1)
                for c in range(HC):
                    k = hf * HC + c
                    for b in range(B):
                        n = b * HC + c
                        dve.wait_ge(c_x[b], k + 1)
                        nc.vector.tensor_tensor(Wd[:, n, 0:DV], Wd[:, n, 0:DV], bank(2 + b)[:, 0:DV],
                                                ALU.subtract).then_inc(c_u[b], 1)
                    for b in range(B):
                        n = b * HC + c
                        dve.wait_ge(c_sp[b], k + 1)
                        if k >= 1:
                            dve.wait_ge(c_o[b], k)
                            dve.wait_ge(c_s[b], k)
                        nc.vector.scalar_tensor_tensor(Sx[:, b, (k + 1) % 2, :], Sx[:, b, k % 2, :],
                                                       sm[:, 7, n:n + 1],
                                                       bank(4 + b)[:, 0:DV], ALU.mult, ALU.add).then_inc(c_s[b], 1)
                dve.wait_ge(c_oe, 4 * hf + 4)
                o2 = R[:, :, 0:DV]
                v.fence(nc.vector.tensor_tensor(o2, Os[:, :, 0:DV], Os[:, :, 0:DV], ALU.mult))
                v.fence(nc.vector.tensor_reduce(sm[:, 11, :], o2, AX.X, ALU.add))
                nc.vector.tensor_scalar(sm[:, 11, :], sm[:, 11, :], 1.0 / DV, EPS, ALU.mult, ALU.add).then_inc(c_os, 1)
                dve.wait_ge(c_gw, hf + 1)
                g0 = 2 * DK + DV
                v.fence(nc.vector.tensor_tensor(Os[:, :, 0:DV], Os[:, :, 0:DV], PJ[:, :, g0:g0 + DV], ALU.mult))
                dve.wait_ge(c_or, hf + 1)
                v.fence(nc.vector.tensor_tensor(Os[:, :, 0:DV], Os[:, :, 0:DV], rowwise(sm[:, 12, :], DV), ALU.mult))
                v.fence(nc.vector.transpose(OT0[:, :, :], Os[:, :, 0:32]))
                nc.vector.transpose(OT1[:, :, :], Os[:, :, 32:64]).then_inc(c_ot, 1)
                for b in range(B):
                    dve.wait_ge(c_f, 2 * hf + b + 1)
                    k0 = b * BPB + hf * 4
                    x = X[:, k0:k0 + 4, :].rearrange("p k d -> p (k d)")
                    nc.vector.tensor_tensor(x, bank(4 + b), x, ALU.add).then_inc(c_fx, 1)

        cctx.close()

        WT = sb("WT", [P, 3, D], F32)
        XP = sb("XP", [P, B, 1 + S], F32)
        XPW = sb("XPW", [P, 2, 2, 512], F32)
        XM = sb("XM", [P, 2, NT], F32)
        KA = sb("KA", [P, NT], F32)
        SG = sb("SG", [P, NB, D], F32)

        d_pad = sem("d_pad")
        d_om = sem("d_om")
        d_wt = sem("d_wt")
        d_wc = sem("d_wc")
        d_sh = sem("d_sh")
        d_mx = sem("d_mx")
        d_r = sem("d_r")
        d_sg = sem("d_sg")
        d_k = sem("d_k")
        d_ka = sem("d_ka")
        d_v = sem("d_v")
        d_g = sem("d_g")
        d_x = sem("d_x")

        def d_sync(sp):
            for q in range(4):
                sp.wait_ge(d_x, q + 1)
                sp.dma_start(out_tok[:, 4 * q:4 * q + 4, :], X[:, 4 * q:4 * q + 4, :]).then_inc(s_out, 16)
            sp.wait_ge(s_out, 64)

        def d_pool(pool):
            pool.wait_ge(c_fx, 4)
            nc.gpsimd.memset(XP[:, :, 0:1], 0.0).then_inc(d_pad, 1)
            for q in range(4):
                ln_power(pool, 3, q)

        def d_pe(pe):
            pe.wait_ge(c_fx, 4)
            pe.wait_ge(d_ld, 80)
            for i in range(3):
                mm = nc.tensor.transpose(bank(4)[:, i * P:(i + 1) * P], Wn[:, i, :], ident[:, :])
            mm.then_inc(d_wt, 1)
            for q in range(4):
                ln_transpose(pe, 3, q, q)
            pe.wait_ge(d_wc, 1)
            for q in range(5):
                if q < 4:
                    cols = slice(512 * q, 512 * q + 512)
                    pe.wait_ge(d_mx, 2 * q + 1)
                    for j in range(4):
                        c0 = 512 * q + j * P
                        mm = nc.tensor.matmul(bank(q)[:, j * P:(j + 1) * P], XM[:, 0, c0:c0 + P], WT[:, 0, :],
                                              start=True, stop=True)
                    mm.then_inc(d_r, 1)
                    pe.wait_ge(d_mx, 2 * q + 2)
                    if q >= 2:
                        pe.wait_ge(d_ka, q - 1)
                    nc.tensor.matmul(bank(4 + q % 2), WT[:, 1, :], XM[:, 1, cols], start=True, stop=True).then_inc(d_k, 1)
                if q >= 1:
                    pe.wait_ge(d_ka, q)
                    if q >= 3:
                        pe.wait_ge(d_g, q - 2)
                    for j in range(4):
                        c0 = 512 * (q - 1) + j * P
                        mm = nc.tensor.matmul(bank(6 + (q - 1) % 2)[:, j * P:(j + 1) * P], KA[:, c0:c0 + P],
                                              WT[:, 2, :], start=True, stop=True)
                    mm.then_inc(d_v, 1)

        def d_act(act):
            act.wait_ge(d_wt, 1)
            nc.scalar.activation(WT[:, :, :].rearrange("p i d -> p (i d)"), bank(4)[:, 0:3 * P],
                                 ACT.Copy).then_inc(d_wc, 1)
            for q in range(5):
                if q < 4:
                    b, o = divmod(512 * q, S)
                    act.wait_ge(ln_tr, 12 + q + 1)
                    nc.scalar.activation(XP[:, b, 1 + o:1 + o + 512], bank(q), ACT.Copy).then_inc(ln_xt, 1)
                    act.wait_ge(ln_xt, 12 + q + 1)
                    act.wait_ge(d_om, 1)
                    act.wait_ge(d_pad, 1)
                    if q >= 2:
                        act.wait_ge(d_mx, 2 * q - 2)
                    for w in range(2):
                        nc.scalar.activation(XPW[:, w, q % 2, :], XP[:, b, o:o + 512], ACT.Copy,
                                             scale=om[:, w:w + 1]).then_inc(d_sh, 1)
                if q >= 1:
                    act.wait_ge(d_r, q)
                    nc.scalar.activation(SG[:, 4 * q - 4:4 * q, :].rearrange("p k d -> p (k d)"), bank(q - 1),
                                         ACT.Sigmoid).then_inc(d_sg, 1)

        def d_dve(dve, v):
            dve.wait_ge(c_fx, 4)
            dve.wait_ge(d_ld, 80)
            nc.vector.tensor_scalar(om[:, :], mu[:, :], -1.0, 1.0, ALU.mult, ALU.add).then_inc(d_om, 1)
            for q in range(4):
                ln_stats(v, q)
            for q in range(4):
                ln_apply(dve, 3, q)
            for q in range(6):
                if q < 4:
                    b, o = divmod(512 * q, S)
                    for w in range(2):
                        dve.wait_ge(d_sh, 2 * q + w + 1)
                        nc.vector.scalar_tensor_tensor(XM[:, w, 512 * q:512 * q + 512], XP[:, b, 1 + o:1 + o + 512],
                                                       mu[:, w:w + 1], XPW[:, w, q % 2, :],
                                                       ALU.mult, ALU.add).then_inc(d_mx, 1)
                if 1 <= q <= 4:
                    dve.wait_ge(d_k, q)
                    k = KA[:, 512 * (q - 1):512 * q]
                    v.fence(nc.vector.tensor_scalar(k, bank(4 + (q - 1) % 2), 0.0, None, ALU.max))
                    nc.vector.tensor_tensor(k, k, k, ALU.mult).then_inc(d_ka, 1)
                if q >= 2:
                    n = q - 2
                    g = SG[:, 4 * n:4 * n + 4, :].rearrange("p k d -> p (k d)")
                    x = X[:, 4 * n:4 * n + 4, :].rearrange("p k d -> p (k d)")
                    dve.wait_ge(d_v, n + 1)
                    dve.wait_ge(d_sg, n + 1)
                    nc.vector.tensor_tensor(g, bank(6 + n % 2), g, ALU.mult).then_inc(d_g, 1)
                    dve.wait_ge(d_g, n + 1)
                    nc.vector.tensor_tensor(x, x, g, ALU.add).then_inc(d_x, 1)

        block = ctx.enter_context(nc.Block())

        @block.sync
        def _(sp):
            loads(sp)
            a_sync(sp)
            b_sync(sp)
            c_loads(sp)
            d_sync(sp)

        @block.gpsimd
        def _(pool):
            c = Count(pool, s_pool)
            a_pool(pool, c)
            b_pool(pool, c)
            c_pool(pool, c)
            d_pool(pool)

        @block.scalar
        def _(act):
            a_act(act)
            b_act(act)
            c_act(act, Count(act, s_act))
            d_act(act)

        @block.tensor
        def _(pe):
            a_pe(pe)
            b_pe(pe)
            c_pe(pe)
            d_pe(pe)

        @block.vector
        def _(dve):
            v = Count(dve, s_dve)
            a_dve(dve, v)
            b_dve(dve, v)
            c_dve(dve, v)
            d_dve(dve, v)


def kernel(**inputs):
    import numpy as _np
    import concourse.bacc as _bacc
    from concourse import mybir as _mybir
    from concourse.bass_utils import run_bass_kernel_spmd as _run

    nc = _bacc.Bacc("TRN2", target_bir_lowering=False, num_devices=1)
    arrays, tensors = {}, {}
    for name in inputs:
        a = _np.ascontiguousarray(inputs[name])
        arrays[f"in_{name}_dram"] = a
        tensors[name] = nc.dram_tensor(f"in_{name}_dram", a.shape, _mybir.dt.from_np(a.dtype),
                                       kind="ExternalInput").ap()
    tensors["out"] = nc.dram_tensor("out_0_dram", (B, S, D), _mybir.dt.float32, kind="ExternalOutput").ap()
    program(nc, tensors)
    r = _run(nc, [arrays], core_ids=[0])
    return r.results[0]["out_0_dram"]
```

```python
from contextlib import ExitStack

import concourse.bass as bass
from concourse import mybir

F32 = mybir.dt.float32
BF16 = mybir.dt.bfloat16
I32 = mybir.dt.int32
U32 = mybir.dt.uint32
ALU = mybir.AluOpType
ACT = mybir.ActivationFunctionType
AX = mybir.AxisListType

P = 128
B, S, D = 2, 1024, 128
NT = B * S
NB = NT // P
BPB = S // P
EPS = 1e-5

H, HD = 16, 8
HG = 4
GR = H // HG
NU = B * GR
SCALE = HD ** -0.5
NPART = 3
Q_TERM = [0, 0, 0, 1, 1, 2]
K_TERM = [0, 1, 2, 0, 1, 0]
NTERM = len(Q_TERM)
KROWS = NTERM * HD
KROWS_M = KROWS + NPART
MASK_VAL = -50000.0
TWO_ONES = 1.0 + 0x3F80 / 2 ** 23

E, FF = 16, 512
CAP = -(-NT // E)
FC = FF // P
WSLOT = 4

CH = 32
NC = S // CH
GH, DK, DV = 4, 24, 48


def score_tiles():
    for a in range(HG // 2):
        for qb in range(BPB):
            n = (qb + 1) * P
            for k0 in range(0, n, 512):
                for j in range(2):
                    yield a, j, qb, k0, min(512, n - k0)


def prob_tiles():
    for c in range(S // 512):
        for kb in range(4 * c + 4):
            q0 = max(kb * P, c * 512)
            yield c, kb, q0, (c + 1) * 512 - q0


STILES = list(score_tiles())
PTILES = list(prob_tiles())
DIAG = 2 * sum(q0 == kb * P for c, kb, q0, w in PTILES)
NS = len(STILES)
NPT = len(PTILES)
C0T = 4
S_COLS = sum(x[4] for x in STILES)
LEAD = 4096

SLOTS = [(kind, i, k) for i in range(NPT) for kind in ("probs", "values") for k in range(4)]


def v_part(i, k):
    c, kb, q0, w = PTILES[i]
    first = q0 - c * 512
    if kb == 0:
        return (first, 512) if k == 3 else (first, first)
    return (k * P, k * P + P) if k * P >= first else (first, first)


def slot_cost(kind, i, k):
    if kind == "probs":
        return PTILES[i][3]
    lo, hi = v_part((i - 1) % NPT, k)
    return 4 * (hi - lo)


def score_schedule():
    ahead, cols = 0, 0
    while cols < LEAD:
        cols += STILES[ahead][4]
        ahead += 1
    total = sum(slot_cost(*x) for x in SLOTS)
    counts, done, cost, cols = [], 0, 0, 0
    for x in SLOTS:
        cost += slot_cost(*x)
        while done < NS and cols + STILES[(ahead + done) % NS][4] / 2 <= S_COLS * cost / total:
            cols += STILES[(ahead + done) % NS][4]
            done += 1
        counts.append(done)
    assert done == NS
    return ahead, counts


AHEAD, SENT = score_schedule()
LAST = NS - AHEAD
TURN = {1: SLOTS.index(("values", 1, 3)), 0: SLOTS.index(("values", 5, 3))}
SPREAD = {1: SLOTS.index(("probs", 3, 3)), 0: SLOTS.index(("probs", 7, 3))}
PROJECT = SLOTS.index(("values", 3, 0))
TMAX = min(s for s in range(len(SLOTS)) if SENT[s] >= LAST) + 4
TMAX_PAIR = max(2 * i + k // 2 for kind, i, k in SLOTS[:TMAX + 1] if kind == "probs" and k % 2)




class Count:

    def __init__(self, eng, sem):
        self.eng, self.sem, self.n = eng, sem, 0

    def fence(self, ins):
        self.n += 1
        ins.then_inc(self.sem, 1)
        self.eng.wait_ge(self.sem, self.n)


def program(nc, t):
    ctx = ExitStack()
    with ctx:
        def sb(name, shape, dt, stack=ctx):
            return stack.enter_context(nc.sbuf_tensor(name, shape, dt))

        def sem(name):
            return ctx.enter_context(nc.semaphore(name))

        ps = ctx.enter_context(nc.psum_tensor("ps", [P, 8, 512], F32))

        def bank(i):
            return ps[:, i, :]

        X = sb("X", [P, NB, D], F32)
        XN = sb("XN", [P, NB, D], F32)
        XT = sb("XT", [P, NT], F32)
        bst = sb("bst", [P, NB, 6], F32)
        mv = sb("mv", [P, NB, 2], F32)
        ve = sb("ve", [P, NB], F32)
        rstd = sb("rstd", [P, NB], F32)
        neghalf = sb("neghalf", [P, 2 * NB * B], F32)
        ident = sb("ident", [P, P], F32)
        identb = sb("identb", [P, P], BF16)
        ones = sb("ones", [P, P], F32)

        x_tok = t["L0_attn_x"].rearrange("b (k p) d -> p (b k) d", p=P)
        out_tok = t["out"].rearrange("b (k p) d -> p (b k) d", p=P)

        ld_x = [sem(f"ld_x{i}") for i in range(4)]
        ld_w = sem("ld_w")
        cst = sem("cst")
        ln_var = sem("ln_var")
        ln_rstd = sem("ln_rstd")
        ln_xn = sem("ln_xn")
        ln_tr = sem("ln_tr")
        ln_xt = sem("ln_xt")
        s_dve, s_act, s_pool = sem("s_dve"), sem("s_act"), sem("s_pool")
        s_out = sem("s_out")

        def ln_stats(v, q):
            for j in range(4 * q, 4 * q + 4):
                i = nc.vector.bn_stats(bst[:, j, :], X[:, j, :])
            v.fence(i)
            for j in range(4 * q, 4 * q + 4):
                i = nc.vector.bn_aggr(mv[:, j, :], bst[:, j, :])
            v.fence(i)
            nc.vector.tensor_scalar(ve[:, 4 * q:4 * q + 4], mv[:, 4 * q:4 * q + 4, 1], EPS, None,
                                    ALU.add).then_inc(ln_var, 1)

        def ln_power(pool, k, q):
            pool.wait_ge(ln_var, 4 * k + q + 1)
            nc.gpsimd.tensor_tensor(rstd[:, 4 * q:4 * q + 4], ve[:, 4 * q:4 * q + 4],
                                    neghalf[:, 0:4], ALU.pow).then_inc(ln_rstd, 1)

        def ln_apply(dve, k, q):
            dve.wait_ge(ln_rstd, 4 * k + q + 1)
            if k and q == 0:
                dve.wait_ge(ln_tr, 4 * k)
            for j in range(4 * q, 4 * q + 4):
                i = nc.vector.tensor_scalar(XN[:, j, :], X[:, j, :], mv[:, j, 0:1], rstd[:, j:j + 1],
                                            ALU.subtract, ALU.mult)
            i.then_inc(ln_xn, 1)

        def ln_transpose(pe, k, q, b):
            pe.wait_ge(ln_xn, 4 * k + q + 1)
            for j in range(4):
                i = nc.tensor.transpose(bank(b)[:, j * P:(j + 1) * P], XN[:, 4 * q + j, :], ident[:, :])
            i.then_inc(ln_tr, 1)

        def ln_copy(act, k, q, b):
            act.wait_ge(ln_tr, 4 * k + q + 1)
            nc.scalar.activation(XT[:, 512 * q:512 * q + 512], bank(b), ACT.Copy).then_inc(ln_xt, 1)

        W1s = sb("W1s", [P, WSLOT, FF], F32)
        W2s = sb("W2s", [P, WSLOT, FC, D], F32)
        Wg = sb("Wg", [P, E], F32)
        bgr = sb("bgr", [P, E], F32)
        b2t = sb("b2t", [P, E, D], F32)
        b2r = b2t[0:1, :, :]
        b1row = sb("b1row", [E * FC, P], F32)
        zero = sb("zero", [P, D], F32)
        Wn = sb("Wn", [P, 3, D], F32)
        mu = sb("mu", [P, 2], F32)
        om = sb("om", [P, 2], F32)
        d_ld = sem("d_ld")
        places = nc.dram_tensor("places", [2 * NT, D], F32, kind="Internal").ap()
        answers = nc.dram_tensor("answers", [NT, D], F32, kind="Internal").ap()
        b_w = [sem(f"b_w{i}") for i in range(WSLOT)]
        b_cw = sem("b_cw")
        b_zero = sem("b_zero")
        b_fill = sem("b_fill")
        b_y = sem("b_y")

        def expert_weights(sp, e):
            if e >= WSLOT:
                sp.wait_ge(b_y, e - WSLOT + 1)
            s = e % WSLOT
            sp.dma_start(W1s[:, s, :], t["L0_ffn_W1"][e]).then_inc(b_w[s], 16)
            sp.dma_start(W2s[:, s, :, :], t["L0_ffn_W2"][e].rearrange("(c p) d -> p c d", p=P)).then_inc(b_w[s], 16)

        def expert_constants(sp):
            sp.wait_ge(b_zero, 1)
            sp.dma_start(places[0:NT, :].rearrange("(k p) d -> p k d", p=P),
                         zero[:, :].unsqueeze(1).to_broadcast([P, NB, D])).then_inc(b_fill, 16)
            sp.dma_start(Wg[:, :], t["L0_ffn_Wg"]).then_inc(b_cw, 16)
            sp.dma_start(bgr[:, :], t["L0_ffn_bg"].rearrange("(a e) -> a e", a=1).to_broadcast([P, E])).then_inc(b_cw, 16)
            sp.dma_start(b2r[:, :, :], t["L0_ffn_b2"].rearrange("(a e) d -> a e d", a=1)).then_inc(b_cw, 16)
            sp.dma_start(b1row[:, :], t["L0_ffn_b1"].rearrange("e (c p) -> (e c) p", p=P)).then_inc(b_cw, 16)
            for e in range(WSLOT):
                expert_weights(sp, e)
            for i, name in enumerate(("W_r", "W_k", "W_v")):
                sp.dma_start(Wn[:, i, :], t["L1_ffn_" + name]).then_inc(d_ld, 16)
            for i, name in enumerate(("mu_r", "mu_k")):
                sp.dma_start(mu[:, i:i + 1], t["L1_ffn_" + name].rearrange("(p a) -> p a", a=1)).then_inc(d_ld, 16)

        actx = ExitStack()
        Wq = sb("Wq", [P, D], F32, actx)
        Wkv = sb("Wkv", [P, 2 * D], F32, actx)
        WoP = sb("WoP", [P, GR, D], F32, actx)
        selD = sb("selD", [P, HG], F32, actx)
        maskS = sb("maskS", [P, P], BF16, actx)
        QP = sb("QP", [P, NPART, NT], BF16, actx)
        KP = sb("KP", [P, NPART, NT], BF16, actx)
        rem = sb("rem", [P, 3, 512], F32, actx)
        V = sb("V", [P, NB, D], F32, actx)
        QS = sb("QS", [P, GR, HG // 2, S], BF16, actx)
        KS = sb("KS", [P, 2, GR, HG // 2, S], BF16, actx)
        VX = sb("VX", [P, 2, BPB, HG, 32], F32, actx)
        PR = sb("PR", [P, 2, HG, 512], F32, actx)
        mx0 = sb("mx0", [P, 2, 2, HG // 2, BPB], F32, actx)
        mx1 = sb("mx1", [P, 2, 2, HG // 2, BPB // 2], F32, actx)
        m3 = sb("m3", [P, 2, 2, NPART, HG // 2 * BPB], BF16, actx)
        mr = sb("mr", [P, 2, 2, HG // 2 * BPB], F32, actx)
        MT = sb("MT", [NPART * HG * BPB, 2, P], BF16, actx)
        OT = sb("OT", [P, GR, S], F32, actx)
        RC = sb("RC", [P, 2, 4 * HG], F32, actx)
        Dq = nc.dram_tensor("Dq", [H, NTERM, HD, NT], BF16, kind="Internal").ap()
        Dk = nc.dram_tensor("Dk", [H, NTERM, HD, NT], BF16, kind="Internal").ap()

        a_wz = sem("a_wz")
        a_pps = sem("a_pps")
        a_hi = sem("a_hi")
        a_rem = sem("a_rem")
        a_mid = sem("a_mid")
        a_part = sem("a_part")
        a_vps = sem("a_vps")
        a_v = sem("a_v")
        a_dq = sem("a_dq")
        a_dk = sem("a_dk")
        a_stk = [sem(f"a_stk{i}") for i in range(GR)]
        a_s = sem("a_s")
        a_mx = sem("a_mx")
        a_m3 = sem("a_m3")
        a_mtp = sem("a_mtp")
        a_mt = sem("a_mt")
        a_mrow = [sem(f"a_mrow{i}") for i in range(2)]
        a_st = sem("a_st")
        a_p = sem("a_p")
        a_pm = sem("a_pm")
        a_pv = sem("a_pv")
        a_vx = sem("a_vx")
        a_ot = sem("a_ot")
        a_bc = sem("a_bc")
        a_rc = sem("a_rc")
        a_sp = sem("a_sp")
        a_on = sem("a_on")
        a_y = sem("a_y")
        a_x = sem("a_x")

        SB = (0, 1)
        PVB, MB = 6, 7
        LNB = (7, 6)

        def loads(sp):
            for i in range(4):
                sp.dma_start(X[:, 4 * i:4 * i + 4, :], x_tok[:, 4 * i:4 * i + 4, :]).then_inc(ld_x[i], 16)
            sp.dma_start(Wq[:, :], t["L0_attn_Wq"]).then_inc(ld_w, 16)
            sp.dma_start(Wkv[:, :], t["L0_attn_Wkv"]).then_inc(ld_w, 16)
            sp.wait_ge(a_wz, 1)
            wo = t["L0_attn_Wo"].rearrange("(g e d) n -> e d g n", g=GR, e=HG)
            for e in range(HG):
                sp.dma_start(WoP[32 * e:32 * e + HD, :, :], wo[e]).then_inc(ld_w, 16)

        def a_sync(sp):
            for b in range(B):
                sp.wait_ge(a_part, 4 * (b + 1))
                cols = slice(b * S, (b + 1) * S)
                for n in range(NTERM):
                    sp.dma_start(Dq[:, n, :, cols], QP[:, Q_TERM[n], cols]).then_inc(a_dq, 16)
                    sp.dma_start(Dk[:, n, :, cols], KP[:, K_TERM[n], cols]).then_inc(a_dk, 16)
                if b == 0:
                    for u in range(GR):
                        stack_loads(sp, u)
                    expert_constants(sp)
            max_rows(sp, 0)
            for u in range(NU):
                if u + 1 < NU:
                    max_rows(sp, u + 1)
                if u + GR < NU:
                    stack_loads(sp, u + GR)

        def stack_loads(sp, u):
            b, g = divmod(u, GR)
            sp.wait_ge(a_dq, 16 * NTERM * (b + 1))
            sp.wait_ge(a_dk, 16 * NTERM * (b + 1))
            if u == 0:
                sp.wait_ge(a_wz, 4)
            if u == GR:
                sp.wait_ge(b_zero, 1)
            if b:
                sp.wait_ge(a_pv, NPT * (u - GR + 1))
            for j in range(2):
                if b:
                    sp.dma_start(QS[64 * j + KROWS:64 * j + KROWS_M, g, :, :],
                                 zero[0:NPART * HG // 2 * S // (2 * D), :].bitcast(BF16)).then_inc(a_stk[g], 16)
                for dst, src in ((QS, Dq), (KS[:, j], Dk)):
                    sp.dma_start(dst[64 * j:64 * j + KROWS, g, :, :],
                                 src[4 * g + j:4 * g + 4:2, :, :, b * S:(b + 1) * S].rearrange("a n d t -> (n d) a t")
                                 ).then_inc(a_stk[g], 16)

        def max_rows(q, u):
            q.wait_ge(a_mt, u + 1)
            half = NPART * HG // 2 * BPB
            for j in range(2):
                q.dma_start(QS[64 * j + KROWS:64 * j + KROWS_M, u % GR, :, :].rearrange("n a (k p) -> n (a k) p", p=P),
                            MT[half * j:half * j + half, u % 2, :]).then_inc(a_mrow[u % 2], 16)

        def a_pool(pool, c):
            nc.gpsimd.memset(WoP[:, :, :], 0.0).then_inc(a_wz, 1)
            c.fence(nc.gpsimd.memset(ident[:, :], 0.0))
            nc.gpsimd.affine_select(out=ident[:, :], in_=ident[:, :], compare_op=ALU.not_equal, fill=1.0,
                                    base=0, pattern=[[-1, P]], channel_multiplier=1).then_inc(cst, 1)
            nc.gpsimd.memset(neghalf[:, :], -0.5).then_inc(cst, 1)
            for q in range(4):
                if q == 0:
                    pool.wait_ge(cst, 2)
                ln_power(pool, 0, q)
            c.fence(nc.gpsimd.memset(identb[:, :], 0.0))
            nc.gpsimd.affine_select(out=identb[:, :], in_=identb[:, :], compare_op=ALU.not_equal, fill=1.0,
                                    base=0, pattern=[[-1, P]], channel_multiplier=1).then_inc(cst, 1)
            pool.wait_ge(cst, 3)
            c.fence(nc.gpsimd.memset(KS[:, :, :, :, :].rearrange("p j g a s -> p (j g a s)").bitcast(F32), 0.0))
            for j in range(2):
                nc.gpsimd.memset(KS[64 * j + 32:64 * j + 64, j, :, :, :].rearrange("p g a s -> p (g a s)").bitcast(F32),
                                 TWO_ONES).then_inc(a_wz, 1)
                pool.wait_ge(a_wz, j + 2)
            nc.gpsimd.memset(QS[:, :, :, :].rearrange("p g a s -> p (g a s)").bitcast(F32), 0.0).then_inc(a_wz, 1)
            nc.gpsimd.memset(ones[:, :], 1.0).then_inc(cst, 1)
            c.fence(nc.gpsimd.memset(maskS[:, :], 0.0))
            nc.gpsimd.affine_select(out=maskS[:, :], in_=maskS[:, :], compare_op=ALU.is_ge, fill=MASK_VAL,
                                    base=0, pattern=[[-1, P]], channel_multiplier=1).then_inc(cst, 1)
            c.fence(nc.gpsimd.memset(selD[:, :], 0.0))
            nc.gpsimd.affine_select(out=selD[:, :], in_=selD[:, :], compare_op=ALU.not_equal, fill=1.0,
                                    base=-HD, pattern=[[-32, HG]], channel_multiplier=1).then_inc(cst, 1)
            nc.gpsimd.memset(zero[:, :], 0.0).then_inc(b_zero, 1)
            c.fence(nc.gpsimd.memset(VX[:, :, :, :, :], 0.0))
            c.fence(nc.gpsimd.memset(VX[:, :, :, :, HD:HD + 1], 1.0))
            widen_v(pool, 0)
            for u in range(NU):
                for n in range(2 * NPT):
                    if n == 2 * 2 and u + 1 < NU:
                        widen_v(pool, u + 1)
                    c, kb, q0, w = PTILES[n // 2]
                    if q0 == kb * P:
                        pool.wait_ge(a_p, 2 * NPT * u + n + 1)
                        o = PR[:, n // 2 % 2, 2 * (n % 2):2 * (n % 2) + 2, 0:P]
                        nc.gpsimd.affine_select(out=o, in_=o, compare_op=ALU.is_ge, fill=0.0, base=0,
                                                pattern=[[0, 2], [1, P]], channel_multiplier=-1).then_inc(a_pm, 1)

        def widen_v(pool, u):
            b, g = divmod(u, GR)
            pool.wait_ge(a_v, 2 * (b + 1))
            if u >= 2:
                pool.wait_ge(a_pv, NPT * (u - 1))
            nc.gpsimd.tensor_copy(
                VX[:, u % 2, :, :, 0:HD],
                V[:, b * BPB:(b + 1) * BPB, 32 * g:32 * g + 32].rearrange("p k (e d) -> p k e d", d=HD),
            ).then_inc(a_vx, 1)

        PIECES = [(c, w) for c in range(4) for w in range(2)]

        def a_pe(pe):
            pe.wait_ge(cst, 2)
            for b in range(B):
                for c in (2 * b, 2 * b + 1):
                    if c >= 2:
                        pe.wait_ge(ln_xt, c - 1)
                    ln_transpose(pe, 0, c, LNB[c % 2])
                if b:
                    values(pe, 0)
                for c in (2 * b, 2 * b + 1):
                    pe.wait_ge(ln_xt, c + 1)
                    if c == 0:
                        pe.wait_ge(ld_w, 96)
                    for w in range(2):
                        n = 2 * c + w
                        if n >= 4:
                            pe.wait_ge(a_part, n - 3)
                        lhs = Wq[:, :] if w == 0 else Wkv[:, 0:D]
                        nc.tensor.matmul(bank(n % 4), lhs, XT[:, 512 * c:512 * c + 512],
                                         start=True, stop=True).then_inc(a_pps, 1)
            values(pe, 1)
            pe.wait_ge(cst, 6)
            pe.wait_ge(a_v, 4)
            for i in range(NS):
                score_piece(pe, 0, i)
            for i in range(AHEAD):
                score_piece(pe, 1, i)
                if i == 1:
                    transpose_max(pe, 0)
            for u in range(NU):
                pe.wait_ge(a_mrow[u % 2], 32 * (u // 2 + 1))
                pe.wait_ge(a_vx, u + 1)
                for s, (kind, i, part) in enumerate(SLOTS):
                    for k in range(SENT[s - 1] if s else 0, SENT[s]):
                        score_piece(pe, *stream(u, k))
                    n = NPT * u + i - 1
                    if kind == "probs":
                        prob_piece(pe, u, 2 * i + part // 2, part % 2)
                    elif n >= 0:
                        times_v(pe, n // NPT, n % NPT, part)
                    if s == TURN[1] and u >= 1:
                        turn_sums(pe, u - 1, 1)
                    if s == SPREAD[1] and u >= 1:
                        spread_sums(pe, u - 1, 1)
                    if PROJECT <= s < PROJECT + BPB and u == GR:
                        project_out(pe, 0, s - PROJECT)
                    if s == TURN[0]:
                        turn_sums(pe, u, 0)
                    if s == SPREAD[0]:
                        spread_sums(pe, u, 0)
                    if s == TMAX and u + 1 < NU:
                        transpose_max(pe, u + 1)
            for part in range(4):
                times_v(pe, NU - 1, NPT - 1, part)
            turn_sums(pe, NU - 1, 1)
            spread_sums(pe, NU - 1, 1)
            for kb in range(BPB):
                project_out(pe, 1, kb)

        def values(pe, b):
            for c in (2 * b, 2 * b + 1):
                if c >= 2:
                    pe.wait_ge(a_v, c - 1)
                for j in range(4):
                    i = nc.tensor.matmul(bank(4 + c % 2)[:, j * P:(j + 1) * P],
                                         XT[:, (4 * c + j) * P:(4 * c + j + 1) * P], Wkv[:, D:2 * D],
                                         start=True, stop=True)
                i.then_inc(a_vps, 1)

        def stream(u, k):
            k += AHEAD
            return u + 1 + k // NS, k % NS

        def score_piece(pe, u, i):
            if u >= NU:
                return
            a, j, qb, k0, n = STILES[i]
            g = u % GR
            if i == 0:
                pe.wait_ge(a_stk[g], 16 * (4 if u < GR else 10))
            m = u * NS + i
            if m >= 2:
                pe.wait_ge(a_mx, m - 1)
            diag = k0 + n == (qb + 1) * P
            o = bank(4 + m % 2)
            mm = nc.tensor.matmul(o[:, 0:n], QS[:, g, a, qb * P:(qb + 1) * P], KS[:, j, g, a, k0:k0 + n],
                                  start=True, stop=not diag)
            if diag:
                mm = nc.tensor.matmul(o[:, n - P:n], identb[:, :], maskS[:, :], start=False, stop=True)
            mm.then_inc(a_s, 1)

        def transpose_max(pe, u):
            pe.wait_ge(a_m3, u + 1)
            if u >= 1:
                pe.wait_ge(a_mt, u)
            if u >= 1:
                pe.wait_ge(a_on, 2 * u - 1)
            nc.tensor.transpose(bank(MB).bitcast(BF16)[0:NPART * HG * BPB, 0:P],
                                m3[:, u % 2, :, :, :].rearrange("p j n k -> p (j n k)"), identb[:, :]).then_inc(a_mtp, 1)

        def prob_piece(pe, u, n, j):
            c, kb, q0, w = PTILES[n // 2]
            m = 2 * NPT * u + n
            if m >= 2 and j == 0:
                pe.wait_ge(a_p, m - 1)
            g = u % GR
            mm = nc.tensor.matmul(bank(2 * (n % 2) + j)[:, 0:w], KS[:, j, g, n % 2, kb * P:(kb + 1) * P],
                                  QS[:, g, n % 2, q0:q0 + w], start=True, stop=True)
            if j:
                mm.then_inc(a_st, 1)

        def times_v(pe, u, i, part):
            c, kb, q0, w = PTILES[i]
            last = 4 * c + 3
            lo, hi = v_part(i, part)
            if lo == hi:
                return
            pe.wait_ge(a_p, 2 * NPT * u + 2 * i + 2)
            if q0 == kb * P:
                pe.wait_ge(a_pm, DIAG * u + 2 * sum(x[2] == x[1] * P for x in PTILES[:i + 1]))
            if kb == 0 and 2 * u + c >= 1:
                pe.wait_ge(a_ot, 2 * u + c)
            first = q0 - c * 512
            for e in range(HG):
                mm = nc.tensor.matmul(bank(PVB)[32 * e:32 * e + 32, lo:hi],
                                      VX[:, u % 2, kb, e, :], PR[:, i % 2, e, lo - first:hi - first],
                                      start=kb == 0, stop=kb == last)
            if hi == 512:
                mm.then_inc(a_pv, 1)

        def turn_sums(pe, u, c):
            n = 2 * u + c
            pe.wait_ge(a_ot, n + 1)
            pe.wait_ge(a_mt, min(u + 1 + c, NU))
            if n >= 1:
                pe.wait_ge(a_on, n)
            if n == 2 * GR:
                pe.wait_ge(a_x, 2)
            for j in range(4):
                q0 = c * 512 + j * P
                mm = nc.tensor.matmul(bank(MB)[:, HG * j:HG * j + HG], OT[:, u % GR, q0:q0 + P], selD[:, :],
                                      start=True, stop=True)
            mm.then_inc(a_bc, 1)

        def spread_sums(pe, u, c):
            n = 2 * u + c
            pe.wait_ge(a_rc, n + 1)
            for j in range(4):
                for e in range(HG):
                    r = RC[:, n % 2, HG * j + e:HG * j + e + 1].to_broadcast([P, 32])
                    mm = nc.tensor.matmul(bank(MB)[32 * e:32 * e + 32, j * P:(j + 1) * P], r, ident[:, :],
                                          start=True, stop=True)
            mm.then_inc(a_sp, 1)

        def project_out(pe, b, kb):
            k, j = divmod(kb, 4)
            if j == 0:
                pe.wait_ge(a_on, 8 * (b + 1))
                if k or b:
                    pe.wait_ge(a_x, 2 * b + k)
            for g in range(GR):
                mm = nc.tensor.matmul(bank(MB)[:, j * P:(j + 1) * P], OT[:, g, kb * P:(kb + 1) * P],
                                      WoP[:, g, :], start=g == 0, stop=g == GR - 1)
            if j == 3:
                mm.then_inc(a_y, 1)

        def a_act(act):
            for n in range(len(PIECES) + 1):
                if n in (0, 4):
                    if n:
                        part_mid(act, n - 1)
                    for q in (n // 2, n // 2 + 1):
                        ln_copy(act, 0, q, LNB[q % 2])
                if n < len(PIECES):
                    part_hi(act, n)
                if n >= 1 and n != 4:
                    part_mid(act, n - 1)
                for q in {5: (0,), 6: (1,), 8: (2, 3)}.get(n, ()):
                    act.wait_ge(a_vps, q + 1)
                    nc.scalar.activation(V[:, 4 * q:4 * q + 4, :].rearrange("p k d -> p (k d)"),
                                         bank(4 + q % 2), ACT.Copy).then_inc(a_v, 1)
            copy_max(act, 0)
            for u in range(NU):
                for n in range(2 * NPT):
                    m = 2 * NPT * u + n
                    i = n // 2
                    c, kb, q0, w = PTILES[i]
                    if kb == 1 and n % 2 == 0 and c == 1:
                        copy_out(act, u, 0)
                    if kb == 1 and n % 2 == 0 and c == 0 and u >= 1:
                        copy_out(act, u - 1, 1)
                    act.wait_ge(a_st, m + 1)
                    if NPT * u + i >= 2:
                        act.wait_ge(a_pv, NPT * u + i - 1)
                    nc.scalar.activation(PR[:, i % 2, 2 * (n % 2):2 * (n % 2) + 2, 0:w],
                                         ps[:, 2 * (n % 2):2 * (n % 2) + 2, 0:w], ACT.Exp).then_inc(a_p, 1)
                    if n == TMAX_PAIR and u + 1 < NU:
                        copy_max(act, u + 1)
            copy_out(act, NU - 1, 1)

        def dst_parts(n):
            c, w = PIECES[n]
            return (QP if w == 0 else KP), slice(512 * c, 512 * c + 512), (SCALE if w == 0 else 1.0)

        def part_hi(act, n):
            dst, cols, s = dst_parts(n)
            act.wait_ge(a_pps, n + 1)
            nc.scalar.activation(dst[:, 0, cols], bank(n % 4), ACT.Copy, scale=s).then_inc(a_hi, 1)

        def part_mid(act, n):
            dst, cols, s = dst_parts(n)
            act.wait_ge(a_rem, n + 1)
            nc.scalar.activation(dst[:, 1, cols], rem[:, n % 3, :], ACT.Copy).then_inc(a_mid, 1)

        def copy_max(act, u):
            act.wait_ge(a_mtp, u + 1)
            if u >= 2:
                act.wait_ge(a_mrow[u % 2], 32 * (u // 2))
            nc.scalar.activation(MT[:, u % 2, :], bank(MB).bitcast(BF16)[0:NPART * HG * BPB, 0:P],
                                 ACT.Copy).then_inc(a_mt, 1)

        def copy_out(act, u, c):
            act.wait_ge(a_pv, NPT * u + (C0T if c == 0 else NPT))
            if u == GR:
                act.wait_ge(a_y, 2)
            nc.scalar.activation(OT[:, u % GR, c * 512:c * 512 + 512], bank(PVB), ACT.Copy).then_inc(a_ot, 1)

        def a_dve(dve, v):
            for q in range(4):
                dve.wait_ge(ld_x[q], 16)
                ln_stats(v, q)
            for q in range(4):
                ln_apply(dve, 0, q)
            for n in range(len(PIECES) + 1):
                if n == 4:
                    part_low(dve, n - 1)
                if n < len(PIECES):
                    dst, cols, s = dst_parts(n)
                    dve.wait_ge(a_hi, n + 1)
                    if n >= 3:
                        dve.wait_ge(a_part, n - 2)
                    nc.vector.scalar_tensor_tensor(rem[:, n % 3, :], bank(n % 4), s, dst[:, 0, cols],
                                                   ALU.mult, ALU.subtract).then_inc(a_rem, 1)
                if n >= 1 and n != 4:
                    part_low(dve, n - 1)
            for i in range(NS):
                reduce_piece(dve, 0, i)
            unit_max(dve, v, 0)
            for i in range(AHEAD):
                reduce_piece(dve, 1, i)
            for u in range(NU):
                for k in range(NS + 1):
                    if k == LAST and u + 1 < NU:
                        unit_max(dve, v, u + 1)
                    if k == SENT[TURN[1]] and u >= 1:
                        reciprocal(dve, u - 1, 1)
                    if k == SENT[SPREAD[1]] and u >= 1:
                        normalise(dve, u - 1, 1)
                    for i in range(2):
                        if k == SENT[PROJECT + 4 * i + 3] and u == GR:
                            residual(dve, 0, i)
                    if k == SENT[TURN[0]]:
                        reciprocal(dve, u, 0)
                    if k == SENT[SPREAD[0]]:
                        normalise(dve, u, 0)
                    if k < NS:
                        reduce_piece(dve, *stream(u, k))
            reciprocal(dve, NU - 1, 1)
            normalise(dve, NU - 1, 1)
            for k in range(2):
                residual(dve, 1, k)

        def part_low(dve, n):
            dst, cols, s = dst_parts(n)
            dve.wait_ge(a_mid, n + 1)
            nc.vector.tensor_tensor(dst[:, 2, cols], rem[:, n % 3, :], dst[:, 1, cols],
                                    ALU.subtract).then_inc(a_part, 1)

        def reduce_piece(dve, u, i):
            if u >= NU:
                return
            a, j, qb, k0, n = STILES[i]
            m = u * NS + i
            if i == 0 and u >= 2:
                dve.wait_ge(a_mtp, u - 1)
            dve.wait_ge(a_s, m + 1)
            o = mx0[:, u % 2, j, a, qb:qb + 1] if k0 == 0 else mx1[:, u % 2, j, a, qb - 4:qb - 3]
            nc.vector.tensor_reduce(o, bank(4 + m % 2)[:, 0:n], AX.X, ALU.max).then_inc(a_mx, 1)

        def unit_max(dve, v, u):
            r = u % 2
            dve.wait_ge(a_mx, NS * (u + 1))
            v.fence(nc.vector.tensor_tensor(mx0[:, r, :, :, 4:8], mx0[:, r, :, :, 4:8], mx1[:, r, :, :, :], ALU.max))
            m = mx0[:, r, :, :, :].rearrange("p j a k -> p j (a k)")
            v.fence(nc.vector.tensor_scalar(m3[:, r, :, 0, :], m, -1.0, None, ALU.mult))
            v.fence(nc.vector.scalar_tensor_tensor(mr[:, r, :, :], m, -1.0, m3[:, r, :, 0, :], ALU.mult, ALU.subtract))
            v.fence(nc.vector.tensor_copy(m3[:, r, :, 1, :], mr[:, r, :, :]))
            nc.vector.tensor_tensor(m3[:, r, :, 2, :], mr[:, r, :, :], m3[:, r, :, 1, :], ALU.subtract).then_inc(a_m3, 1)

        def reciprocal(dve, u, c):
            n = 2 * u + c
            dve.wait_ge(a_bc, n + 1)
            nc.vector.reciprocal(RC[:, n % 2, :], bank(MB)[:, 0:4 * HG]).then_inc(a_rc, 1)

        def normalise(dve, u, c):
            n = 2 * u + c
            dve.wait_ge(a_sp, n + 1)
            o = OT[:, u % GR, c * 512:c * 512 + 512]
            nc.vector.tensor_tensor(o, bank(MB), o, ALU.mult).then_inc(a_on, 1)

        def residual(dve, b, k):
            dve.wait_ge(a_y, 2 * b + k + 1)
            x = X[:, 8 * b + 4 * k:8 * b + 4 * k + 4, :].rearrange("p k d -> p (k d)")
            nc.vector.tensor_tensor(x, bank(MB), x, ALU.add).then_inc(a_x, 1)

        actx.close()

        cctx = ExitStack()
        NH = NC // 2 * B
        KTx = sb("KTx", [P, NH, P], F32, cctx)
        QGx = sb("QGx", [P, NH, P], F32, cctx)
        ATx = sb("ATx", [P, NH, P], F32, cctx)
        KDx = sb("KDx", [P, NH, P], F32, cctx)
        W2x = sb("W2x", [P, NH, P], F32, cctx)
        c_z = sem("c_z")
        NPJ = 2 * DK + 2 * DV + 2
        Win = sb("Win", [P, 2 * D], F32, cctx)
        WC = sb("WC", [P, GH, NPJ], F32, cctx)
        wgb = sb("wgb", [P, 2, GH], F32, cctx)
        WS = sb("WS", [P, 2, D], F32, cctx)
        Wou = sb("Wou", [P, 2, D], F32, cctx)
        cw = sb("cw", [P, 2, 4], F32, cctx)
        cb = sb("cb", [P, 2], F32, cctx)
        gn = sb("gn", [P, DV], F32, cctx)
        par = sb("par", [P, 3], F32, cctx)
        c_ld = sem("c_ld")
        c_wz = sem("c_wz")

        def band(h):
            return slice(32 * h, 32 * h + 32)

        def c_loads(sp):
            sp.wait_ge(a_x, 4)
            sp.wait_ge(c_wz, 1)
            T = lambda n: t["L1_attn_" + n]
            jobs = [(Win[:, :], T("W_in"))]
            at = 0
            for name, w in (("W_q", DK), ("W_k", DK), ("W_v", DV), ("W_g", DV)):
                jobs.append((WC[:, :, at:at + w], T(name).rearrange("p (h k) -> p h k", h=GH)))
                at += w
            jobs += [(wgb[:, 0, :], T("W_gk")), (wgb[:, 1, :], T("W_b"))]
            wso = T("W_so")
            for h in range(GH):
                jobs.append((WS[32 * h:32 * h + 32, 0, :], wso[DV * h:DV * h + 32, :]))
                jobs.append((WS[32 * h:32 * h + DV - 32, 1, :], wso[DV * h + 32:DV * h + DV, :]))
                for i, name in enumerate(("A_log", "dt_bias", "b_b")):
                    jobs.append((par[band(h), i:i + 1],
                                 T(name)[h:h + 1].rearrange("(a b) -> a b", a=1).to_broadcast([32, 1])))
            jobs.append((Wou[:, :, :], T("W_out").rearrange("(a p) n -> p a n", p=P)))
            for i, name in enumerate(("x", "z")):
                jobs.append((cw[:, i, :], T(f"conv_{name}_w").rearrange("p a j -> p (a j)")))
                jobs.append((cb[:, i:i + 1], T(f"conv_{name}_b").rearrange("(p a) -> p a", a=1)))
            jobs.append((gn[:, :], T("g_norm_w").rearrange("(a v) -> a v", a=1).to_broadcast([P, DV])))
            for dst, src in jobs:
                sp.dma_start(dst, src).then_inc(c_ld, 16)
        C_LD = 16 * (1 + 6 + 5 * GH + 1 + 4 + 1)


        bctx = ExitStack()
        trib = sb("trib", [P, P], BF16, bctx)
        oneb = sb("oneb", [P, P], BF16, bctx)
        iotae = sb("iotae", [P, NB, E], F32, bctx)
        itok = sb("itok", [P, NB], F32, bctx)
        first = sb("first", [P, E, NB], F32, bctx)
        lg = sb("lg", [P, NB, E], F32, bctx)
        lmax = sb("lmax", [P, NB], F32, bctx)
        lexp = sb("lexp", [P, NB, E], F32, bctx)
        lsum = sb("lsum", [P, NB], F32, bctx)
        gate = sb("gate", [P, NB], F32, bctx)
        cand = sb("cand", [P, NB, E], F32, bctx)
        cmin = sb("cmin", [P, NB], F32, bctx)
        oh = sb("oh", [P, NB, E], BF16, bctx)
        tot = sb("tot", [P, E, NB], F32, bctx)
        run = sb("run", [P, E, NB], F32, bctx)
        pose = sb("pose", [P, NB, E], F32, bctx)
        pos = sb("pos", [P, NB], F32, bctx)
        keep = sb("keep", [P, NB], F32, bctx)
        base = sb("base", [P, NB], F32, bctx)
        tmp = sb("tmp", [P, 2, NB], F32, bctx)
        sidx = sb("sidx", [P, NB], U32, bctx)
        gidx = sb("gidx", [P, NB], U32, bctx)
        b1T = sb("b1T", [P, E * FC], F32, bctx)
        BT = sb("BT", [P, E, D], F32, bctx)
        BTT = sb("BTT", [P, 2, P], F32, bctx)
        hs = sb("hs", [P, 2, FC, P], F32, bctx)
        YS = sb("YS", [P, E, D], F32, bctx)
        G = sb("G", [P, NB, D], F32, bctx)

        b_cst = sem("b_cst")
        b_lg = sem("b_lg")
        b_d = sem("b_d")
        b_e = sem("b_e")
        b_oh = sem("b_oh")
        b_cnt = sem("b_cnt")
        b_idx = sem("b_idx")
        b_sc = sem("b_sc")
        b_ld = [sem(f"b_ld{i}") for i in range(4)]
        b_b1 = sem("b_b1")
        b_t = sem("b_t")
        b_tt = sem("b_tt")
        b_h = sem("b_h")
        b_rv = sem("b_rv")
        b_ra = sem("b_ra")
        b_ys = sem("b_ys")
        b_ans = sem("b_ans")
        b_g = [sem(f"b_g{i}") for i in range(4)]
        b_x = sem("b_x")

        def b_sync(sp):
            c_loads(sp)
            for i in range(4):
                if i == 0:
                    sp.wait_ge(b_sc, 16 * NB)
                sp.dma_start(BT[:, 4 * i:4 * i + 4, :],
                             places[512 * i:512 * i + 512, :].rearrange("(e p) d -> p e d", p=P)
                             ).then_inc(b_ld[i], 16)
            for e in range(E):
                if e >= WSLOT:
                    expert_weights(sp, e)
                if e % 4 == 3 and e >= 2 * WSLOT - 1:
                    answers_out(sp, e // 4 - 1)
            answers_out(sp, 3)

        def answers_out(sp, i):
            sp.wait_ge(b_ys, 4 * i + 4)
            sp.dma_start(answers[512 * i:512 * i + 512, :].rearrange("(e p) d -> p e d", p=P),
                         YS[:, 4 * i:4 * i + 4, :]).then_inc(b_ans, 16)

        def b_pool(pool, c):
            pool.wait_ge(a_x, 4)
            nc.gpsimd.memset(WS[:, :, :], 0.0).then_inc(c_wz, 1)
            c.fence(nc.gpsimd.memset(trib[:, :], 1.0))
            nc.gpsimd.affine_select(out=trib[:, :], in_=trib[:, :], compare_op=ALU.is_gt, fill=0.0,
                                    base=0, pattern=[[1, P]], channel_multiplier=-1).then_inc(b_cst, 1)
            nc.gpsimd.memset(oneb[:, :], 1.0).then_inc(b_cst, 1)
            nc.gpsimd.iota(iotae[:, :, :], pattern=[[0, NB], [1, E]], base=0, channel_multiplier=0,
                           allow_small_or_imprecise_dtypes=True).then_inc(b_cst, 1)
            nc.gpsimd.iota(itok[:, :], pattern=[[P, NB]], base=NT, channel_multiplier=1,
                           allow_small_or_imprecise_dtypes=True).then_inc(b_cst, 1)
            c.fence(nc.gpsimd.memset(first[:, :, :], 1.0))
            nc.gpsimd.memset(first[:, :, 0:1], 0.0).then_inc(b_cst, 1)
            for q in range(4):
                ln_power(pool, 1, q)
            pool.wait_ge(b_idx, 1)
            pool.wait_ge(b_fill, 16)
            for j in range(NB):
                nc.gpsimd.indirect_dma_start(
                    out=places[:, :], out_offset=bass.IndirectOffsetOnAxis(ap=sidx[:, j:j + 1], axis=0),
                    in_=XN[:, j, :], in_offset=None).then_inc(b_sc, 16)
            for x in (KTx, QGx, ATx, KDx, W2x):
                nc.gpsimd.memset(x[:, :, :], 0.0).then_inc(c_z, 1)
            pool.wait_ge(b_ans, 64)
            for j in range(NB):
                if j == 12:
                    ln_power(pool, 2, 0)
                nc.gpsimd.indirect_dma_start(
                    out=G[:, j, :], out_offset=None, in_=answers[:, :],
                    in_offset=bass.IndirectOffsetOnAxis(ap=gidx[:, j:j + 1], axis=0)).then_inc(b_g[j // 4], 16)
            for q in (1, 2, 3):
                ln_power(pool, 2, q)

        def b_pe(pe):
            pe.wait_ge(b_cw, 64)
            for q in range(4):
                ln_transpose(pe, 1, q, (0, 1, 5, 6)[q])
            nc.tensor.transpose(bank(7)[:, 0:E * FC], b1row[:, :], ident[0:E * FC, 0:E * FC]).then_inc(b_b1, 1)
            for j in range(NB):
                if j % 4 == 0:
                    pe.wait_ge(ln_xt, 4 + j // 4 + 1)
                o = bank(2)[:, j * E:(j + 1) * E]
                mm = nc.tensor.matmul(o, XT[:, j * P:(j + 1) * P], Wg[:, :], start=True, stop=True)
            mm.then_inc(b_lg, 1)
            pe.wait_ge(b_oh, 1)
            pe.wait_ge(b_cst, 2)
            ohf = oh[:, :, :].rearrange("p k e -> p (k e)")
            nc.tensor.matmul(bank(3)[:, 0:NB * E], trib[:, :], ohf, start=True, stop=True)
            nc.tensor.matmul(bank(4)[:, 0:NB * E], oneb[:, :], ohf, start=True, stop=True).then_inc(b_cnt, 1)
            expert_turn(pe, 0)
            for e in range(E):
                if e + 1 < E:
                    expert_turn(pe, e + 1)
                pe.wait_ge(b_tt, e + 1)
                pe.wait_ge(b_w[e % WSLOT], 32 * (e // WSLOT + 1))
                if e >= 2:
                    pe.wait_ge(b_ra, e - 1)
                    pe.wait_ge(b_rv, e - 1)
                else:
                    pe.wait_ge(b_idx, 1)
                    pe.wait_ge(b_b1, 2)
                for f in range(FC):
                    mm = nc.tensor.matmul(hidden(e, f),
                                          W1s[:, e % WSLOT, f * P:(f + 1) * P], BTT[:, e % 2, :],
                                          start=True, stop=True)
                mm.then_inc(b_h, 1)
                if e >= 1:
                    expert_answer(pe, e - 1)
            expert_answer(pe, E - 1)

        def hidden(e, f):
            return bank((2, 6)[e % 2] + f // 2)[:, f % 2 * P:(f % 2 + 1) * P]

        def expert_turn(pe, e):
            pe.wait_ge(b_ld[e // 4], 16)
            if e >= 2:
                pe.wait_ge(b_tt, e - 1)
            elif e == 0:
                pe.wait_ge(ln_xt, 8)
            nc.tensor.transpose(bank(e % 2)[:, 0:P], BT[:, e, :], ident[:, :]).then_inc(b_t, 1)

        def expert_answer(pe, e):
            pe.wait_ge(b_ra, e + 1)
            pe.wait_ge(b_rv, e + 1)
            if e >= 2:
                pe.wait_ge(b_ys, e - 1)
            o = bank(4 + e % 2)[:, 0:D]
            for f in range(FC):
                nc.tensor.matmul(o, hs[:, e % 2, f, :], W2s[:, e % WSLOT, f, :], start=f == 0, stop=False)
            nc.tensor.matmul(o, ones[0:1, :], b2r[:, e, :], start=False, stop=True).then_inc(b_y, 1)

        def b_act(act):
            for q in range(4):
                if q == 0:
                    act.wait_ge(a_y, 4)
                ln_copy(act, 1, q, (0, 1, 5, 6)[q])
            act.wait_ge(b_b1, 1)
            nc.scalar.activation(b1T[:, :], bank(7)[:, 0:E * FC], ACT.Copy).then_inc(b_b1, 1)
            act.wait_ge(b_d, 1)
            nc.scalar.activation(lexp[:, :, :], lg[:, :, :], ACT.Exp).then_inc(b_e, 1)
            act.wait_ge(b_b1, 2)
            expert_copy(act, 0)
            for e in range(E):
                if e + 1 < E:
                    expert_copy(act, e + 1)
                act.wait_ge(b_h, e + 1)
                if e >= 2:
                    act.wait_ge(b_y, e - 1)
                for f in (2, 3):
                    i = nc.scalar.activation(hs[:, e % 2, f, :], hidden(e, f), ACT.Relu,
                                             bias=b1T[:, e * FC + f:e * FC + f + 1])
                i.then_inc(b_ra, 1)
                if e >= 1:
                    answer_copy(act, e - 1)
            answer_copy(act, E - 1)

        def expert_copy(act, e):
            act.wait_ge(b_t, e + 1)
            if e >= 2:
                act.wait_ge(b_h, e - 1)
            nc.scalar.activation(BTT[:, e % 2, :], bank(e % 2)[:, 0:P], ACT.Copy).then_inc(b_tt, 1)

        def answer_copy(act, e):
            act.wait_ge(b_y, e + 1)
            nc.scalar.activation(YS[:, e, :], bank(4 + e % 2)[:, 0:D], ACT.Copy).then_inc(b_ys, 1)

        def b_dve(dve, v):
            dve.wait_ge(a_x, 4)
            for q in range(4):
                ln_stats(v, q)
            for q in range(4):
                ln_apply(dve, 1, q)
            dve.wait_ge(b_lg, 1)
            dve.wait_ge(b_cst, 5)
            p3 = bank(2)[:, 0:NB * E].rearrange("p (k e) -> p k e", e=E)

            def over(x):
                return x.unsqueeze(2).to_broadcast([P, NB, E])

            dve.wait_ge(b_cw, 64)
            v.fence(nc.vector.tensor_tensor(lg[:, :, :], p3, bgr[:, :].unsqueeze(1).to_broadcast([P, NB, E]), ALU.add))
            v.fence(nc.vector.tensor_reduce(lmax[:, :], lg[:, :, :], AX.X, ALU.max))
            v.fence(nc.vector.tensor_tensor(lg[:, :, :], lg[:, :, :], over(lmax[:, :]), ALU.subtract))
            i = nc.vector.tensor_scalar(cand[:, :, :], lg[:, :, :], 0.0, -float(E), ALU.is_ge, ALU.mult)
            i.then_inc(b_d, 1)
            dve.wait_ge(b_d, 1)
            v.fence(nc.vector.tensor_tensor(cand[:, :, :], cand[:, :, :], iotae[:, :, :], ALU.add))
            v.fence(nc.vector.tensor_reduce(cmin[:, :], cand[:, :, :], AX.X, ALU.min))
            nc.vector.tensor_tensor(oh[:, :, :], cand[:, :, :], over(cmin[:, :]), ALU.is_equal).then_inc(b_oh, 1)
            dve.wait_ge(b_e, 1)
            v.fence(nc.vector.tensor_reduce(lsum[:, :], lexp[:, :, :], AX.X, ALU.add))
            nc.vector.reciprocal(gate[:, :], lsum[:, :])
            v.fence(nc.vector.tensor_scalar(base[:, :], cmin[:, :], float(E), float(CAP), ALU.add, ALU.mult))
            dve.wait_ge(b_cnt, 1)
            v.fence(nc.vector.tensor_copy(tot[:, :, :], bank(4)[:, 0:NB * E].rearrange("p (k e) -> p e k", e=E)))
            v.fence(nc.vector.tensor_tensor_scan(
                run[:, :, :].rearrange("p e k -> p (e k)"), first[:, :, :].rearrange("p e k -> p (e k)"),
                tot[:, :, :].rearrange("p e k -> p (e k)"), 0.0, ALU.mult, ALU.add))
            v.fence(nc.vector.tensor_tensor(run[:, :, :], run[:, :, :], tot[:, :, :], ALU.subtract))
            v.fence(nc.vector.tensor_tensor(pose[:, :, :], bank(3)[:, 0:NB * E].rearrange("p (k e) -> p k e", e=E),
                                            run[:, :, :].rearrange("p e k -> p k e"), ALU.add))
            v.fence(nc.vector.tensor_tensor(pose[:, :, :], pose[:, :, :], oh[:, :, :], ALU.mult))
            v.fence(nc.vector.tensor_reduce(pos[:, :], pose[:, :, :], AX.X, ALU.add))
            nc.vector.tensor_scalar(keep[:, :], pos[:, :], float(CAP), None, ALU.is_lt)
            nc.vector.tensor_tensor(tmp[:, 0, :], base[:, :], pos[:, :], ALU.add)
            v.fence(nc.vector.tensor_scalar(tmp[:, 1, :], pos[:, :], float(CAP - 1), None, ALU.min))
            nc.vector.tensor_tensor(gidx[:, :], base[:, :], tmp[:, 1, :], ALU.add)
            nc.vector.tensor_tensor(gate[:, :], gate[:, :], keep[:, :], ALU.mult)
            v.fence(nc.vector.tensor_tensor(tmp[:, 0, :], tmp[:, 0, :], itok[:, :], ALU.subtract))
            v.fence(nc.vector.tensor_tensor(tmp[:, 0, :], tmp[:, 0, :], keep[:, :], ALU.mult))
            nc.vector.tensor_tensor(sidx[:, :], tmp[:, 0, :], itok[:, :], ALU.add).then_inc(b_idx, 1)
            dve.wait_ge(b_b1, 2)
            for e in range(E):
                dve.wait_ge(b_h, e + 1)
                if e >= 2:
                    dve.wait_ge(b_y, e - 1)
                for f in (0, 1):
                    i = nc.vector.tensor_scalar(hs[:, e % 2, f, :], hidden(e, f),
                                                b1T[:, e * FC + f:e * FC + f + 1], 0.0, ALU.add, ALU.max)
                i.then_inc(b_rv, 1)
            for q in range(4):
                dve.wait_ge(b_g[q], 64)
                for j in range(4 * q, 4 * q + 4):
                    nc.vector.scalar_tensor_tensor(X[:, j, :], G[:, j, :], gate[:, j:j + 1], X[:, j, :],
                                                   ALU.mult, ALU.add).then_inc(b_x, 1)
                dve.wait_ge(b_x, 4 * q + 4)
                ln_stats(v, q)
                if q == 3:
                    ln_apply(dve, 2, 0)
            for q in (1, 2, 3):
                ln_apply(dve, 2, q)

        bctx.close()

        HT = S // 2
        HC = NC // 2
        PJG = 3
        NG = -(-NH // PJG)
        RW = DV + 32
        RG = 512 // RW
        NR = -(-NH // RG)
        KQ = W1s[:, :, :].rearrange("p a b -> p (a b)").rearrange("p (n c) -> p n c", c=64)
        XS = W2s[:, :, :, :].rearrange("p a b c -> p (a b c)")
        ZS = XN[:, :, :].rearrange("p k d -> p (k d)")
        KN = XT[:, 0:NH * 32].rearrange("p (n k) -> p n k", k=32)
        QN = XT[:, NH * 32:2 * NH * 32].rearrange("p (n k) -> p n k", k=32)
        XC = sb("XC", [P, B, S + 3], F32, cctx)
        ZC = sb("ZC", [P, B, S + 3], F32, cctx)
        PJ = sb("PJ", [P, NH, NPJ], F32, cctx)
        Ed = XC[:, 0, 0:S].rearrange("p (n s) -> p n s", s=32)
        Et = XC[:, 1, 0:S].rearrange("p (n s) -> p n s", s=32)
        Lp = sb("Lp", [P, 32, 32], F32, cctx)
        Mp = sb("Mp", [P, 32, 32], F32, cctx)
        mt = sb("mt", [P, 256], F32, cctx)
        R = sb("R", [P, NH, RW], F32, cctx)
        Wd = sb("Wd", [P, NH, RW], F32, cctx)
        Lc = Wd[:, :, 0:32]
        Os = b2t[:, :, :].rearrange("p e d -> p (e d)").rearrange("p (n v) -> p n v", v=64)
        YT = ZC[:, :, 0:HT]
        Sx = sb("Sx", [P, B, 2, DV], F32, cctx)
        dgw = sb("dgw", [P, 4, P], F32, cctx)
        tri = sb("tri", [P, P], F32, cctx)
        blk = sb("blk", [P, P], F32, cctx)
        dmask = sb("dmask", [P, 32], F32, cctx)
        sm = sb("sm", [P, 16, NH], F32, cctx)
        OT0, OT1 = Ed, Et
        gsum = mt[:, 0:3 * NH].rearrange("p (a n) -> p a n", a=3)
        ss = mt[:, 3 * NH:5 * NH].rearrange("p (n a) -> p n a", a=2)
        rs = mt[:, 5 * NH:7 * NH].rearrange("p (n a) -> p n a", a=2)

        c_cst = sem("c_cst")
        c_xc = sem("c_xc")
        c_xce = sem("c_xce")
        c_pad = sem("c_pad")
        c_wc = sem("c_wc")
        c_dg = sem("c_dg")
        c_cv = sem("c_cv")
        c_xs = sem("c_xs")
        c_zp = sem("c_zp")
        c_zs = sem("c_zs")
        c_pj = sem("c_pj")
        c_pje = sem("c_pje")
        c_ss = sem("c_ss")
        c_rs = sem("c_rs")
        c_n = sem("c_n")
        c_kq = sem("c_kq")
        c_kx = sem("c_kx")
        c_gr = sem("c_gr")
        c_zz = sem("c_zz")
        c_ga = sem("c_ga")
        c_gk = sem("c_gk")
        c_gc = sem("c_gc")
        c_gs = sem("c_gs")
        c_ge = sem("c_ge")
        c_be = sem("c_be")
        c_dd = sem("c_dd")
        c_ed = sem("c_ed")
        c_r = sem("c_r")
        c_kd = sem("c_kd")
        c_qg = sem("c_qg")
        c_qx = sem("c_qx")
        c_at = sem("c_at")
        c_mi = sem("c_mi")
        c_fs = sem("c_fs")
        c_tt = sem("c_tt")
        c_w = sem("c_w")
        c_we = sem("c_we")
        c_w2 = sem("c_w2")
        c_clr = sem("c_clr")
        c_x = [sem(f"c_x{b}") for b in range(B)]
        c_u = [sem(f"c_u{b}") for b in range(B)]
        c_sp = [sem(f"c_sp{b}") for b in range(B)]
        c_s = [sem(f"c_s{b}") for b in range(B)]
        c_o = [sem(f"c_o{b}") for b in range(B)]
        c_oe = sem("c_oe")
        c_gg = sem("c_gg")
        c_gw = sem("c_gw")
        c_os = sem("c_os")
        c_gm = sem("c_gm")
        c_or = sem("c_or")
        c_ot = sem("c_ot")
        c_y = sem("c_y")
        c_ye = sem("c_ye")
        c_f = sem("c_f")
        c_fx = sem("c_fx")

        def rowwise(x, w):
            return x.unsqueeze(2).to_broadcast([x.shape[0], NH, w])

        def c_pool(pool, c):
            pool.wait_ge(b_x, NB)
            pool.wait_ge(c_z, 5)
            for x in (XC, ZC):
                nc.gpsimd.memset(x[:, :, 0:1], 0.0).then_inc(c_pad, 1)
                nc.gpsimd.memset(x[:, :, S + 1:S + 3], 0.0).then_inc(c_pad, 1)
            nc.gpsimd.memset(tri[:, :], 1.0)
            c.fence(nc.gpsimd.memset(blk[:, :], 1.0))
            b4 = lambda x: x[:, :].rearrange("p (h r) -> p h r", h=GH)
            c.fence(nc.gpsimd.affine_select(out=b4(blk), in_=b4(blk), compare_op=ALU.is_ge, fill=0.0, base=0,
                                            pattern=[[-32, GH], [0, 32]], channel_multiplier=1))
            nc.gpsimd.affine_select(out=b4(blk), in_=b4(blk), compare_op=ALU.is_ge, fill=0.0, base=31,
                                    pattern=[[32, GH], [0, 32]], channel_multiplier=-1).then_inc(c_cst, 1)
            c.fence(nc.gpsimd.affine_select(out=tri[:, :], in_=tri[:, :], compare_op=ALU.is_ge, fill=0.0, base=0,
                                            pattern=[[1, P]], channel_multiplier=-1))
            nc.gpsimd.affine_select(out=b4(tri), in_=b4(tri), compare_op=ALU.is_ge, fill=0.0, base=0,
                                    pattern=[[-32, GH], [0, 32]], channel_multiplier=1).then_inc(c_cst, 1)
            c.fence(nc.gpsimd.memset(dmask[:, :], 0.0))
            for h in range(GH):
                c.fence(nc.gpsimd.affine_select(out=dmask[band(h), :], in_=dmask[band(h), :], compare_op=ALU.is_ge,
                                                fill=-1e30, base=0, pattern=[[-1, 32]], channel_multiplier=1))
            c.fence(nc.gpsimd.memset(Os[:, :, DV:64], 0.0))
            c.fence(nc.gpsimd.memset(R[:, :, DV + DK:RW], 0.0))
            nc.gpsimd.memset(Sx[:, :, :, :], 0.0).then_inc(c_clr, 1)
            for hf in range(2):
                if hf == 0:
                    pool.wait_ge(c_xce, 8)
                    nc.gpsimd.memset(KN[:, :, DK:32], 0.0).then_inc(c_clr, 1)
                    nc.gpsimd.memset(QN[:, :, DK:32], 0.0).then_inc(c_clr, 1)
                if hf:
                    pool.wait_ge(c_tt, 1)
                c.fence(nc.gpsimd.memset(Mp[:, :, :], 0.0))
                nc.gpsimd.memset(Mp[:, :, :].rearrange("p t s -> p (t s)")[:, 0:32 * 32:33], 1.0).then_inc(c_mi, 1)
                pool.wait_ge(c_kq, hf + 1)
                pool.wait_ge(c_mi, hf + 1)
                pool.wait_ge(c_kq, hf + 1)
                pool.wait_ge(c_n, hf + 1)
                pool.wait_ge(c_ge, hf + 1)
                pool.wait_ge(c_be, hf + 1)
                if hf:
                    for b in range(B):
                        pool.wait_ge(c_o[b], HC)
                    pool.wait_ge(c_os, 1)
                nc.gpsimd.tensor_tensor(QN[:, :, 0:DK], QN[:, :, 0:DK], rowwise(sm[:, 5, :], DK), ALU.mult
                                        ).then_inc(c_qg, 1)
                nc.gpsimd.tensor_tensor(R[:, :, 0:DV], PJ[:, :, 2 * DK:2 * DK + DV], rowwise(sm[:, 8, :], DV),
                                        ALU.mult).then_inc(c_r, 1)
                nc.gpsimd.tensor_tensor(R[:, :, DV:DV + DK], KN[:, :, 0:DK], rowwise(sm[:, 9, :], DK),
                                        ALU.mult).then_inc(c_r, 1)
                pool.wait_ge(c_r, 2 * hf + 2)
                for h in range(GH):
                    i = nc.gpsimd.tensor_tensor(KDx[band(h), :, 32 * h:32 * h + DK], KN[band(h), :, 0:DK],
                                                rowwise(sm[band(h), 6, :], DK), ALU.mult)
                    i.then_inc(c_kd, 1)
                    pool.wait_ge(c_kd, GH * hf + h + 1)
                pool.wait_ge(c_gg, hf + 1)
                nc.gpsimd.tensor_tensor(PJ[:, :, 2 * DK + DV:2 * DK + 2 * DV], PJ[:, :, 2 * DK + DV:2 * DK + 2 * DV],
                                        gn[:, :].unsqueeze(1).to_broadcast([P, NH, DV]), ALU.mult).then_inc(c_gw, 1)

        def c_pe(pe):
            for q in range(4):
                ln_transpose(pe, 2, q, (0, 1, 2, 3)[q])
            pe.wait_ge(c_ld, C_LD)
            pe.wait_ge(b_ys, E)
            for q in range(4):
                pe.wait_ge(ln_xt, 8 + q + 1)
                for w in range(2):
                    n = 2 * q + w
                    if n >= 4:
                        pe.wait_ge(c_xce, n - 3)
                    nc.tensor.matmul(bank(4 + n % 4), Win[:, w * D:(w + 1) * D], XT[:, 512 * q:512 * q + 512],
                                     start=True, stop=True).then_inc(c_xc, 1)
            for hf in range(2):
                if hf == 0:
                    project_chunks(pe, 0)
                pe.wait_ge(c_gk, hf + 1)
                pe.wait_ge(c_cst, 2)
                if hf == 1:
                    pe.wait_ge(c_oe, 4)
                nc.tensor.matmul(bank(6)[:, 0:NH], tri[:, :], sm[:, 2, :], start=True, stop=True)
                nc.tensor.matmul(bank(6)[:, NH:2 * NH], blk[:, :], sm[:, 2, :], start=True, stop=True).then_inc(c_gc, 1)
                pe.wait_ge(c_n, hf + 1)
                keep_clock(96, 7)
                pe.wait_ge(c_kx, GH * (hf + 1))
                if hf == 1:
                    pe.wait_ge(c_fx, 2)
                    pe.wait_ge(c_ye, 2)
                for n in range(NH):
                    mm = nc.tensor.matmul(bank(2 + n // 8)[:, n % 8 * 64:(n % 8 + 1) * 64], KTx[:, n, :], KQ[:, n, :],
                                          start=True, stop=True)
                    if n % 8 == 7:
                        mm.then_inc(c_gr, 1)
                if hf == 0:
                    pe.wait_ge(c_dg, 1)
                    pe.wait_ge(c_xce, 8)
                    pe.wait_ge(c_gs, 1)
                    for q in range(4):
                        b, o = divmod(512 * q, S)
                        if q >= 1:
                            pe.wait_ge(c_zs, q)
                        for j in range(4):
                            mm = nc.tensor.matmul(bank(7), dgw[:, j, :], ZC[:, b, o + j:o + j + 512],
                                                  start=j == 0, stop=j == 3)
                        mm.then_inc(c_zp, 1)
                pe.wait_ge(c_fs, hf + 1)
                keep_clock(80, 6)
                pe.wait_ge(c_tt, hf + 1)
                pe.wait_ge(c_r, 2 * hf + 2)
                for g in range(NR):
                    m = hf * NR + g
                    if g == 0:
                        pe.wait_ge(c_pje, NG * (hf + 1))
                    if m >= 2:
                        pe.wait_ge(c_we, m - 1)
                    for i in range(min(RG, NH - RG * g)):
                        n = RG * g + i
                        mm = nc.tensor.matmul(bank(g % 2)[:, i * RW:(i + 1) * RW], KTx[:, n, :], R[:, n, :],
                                              start=True, stop=True)
                    mm.then_inc(c_w, 1)
                keep_clock(48, 6)
                pe.wait_ge(c_w2, hf + 1)
                pe.wait_ge(c_kd, GH * (hf + 1))
                pe.wait_ge(c_qx, hf + 1)
                pe.wait_ge(c_clr, 1)
                pe.wait_ge(c_we, NR * (hf + 1))
                pe.wait_ge(c_zs, 4)
                pe.wait_ge(c_at, hf + 1)
                for c in range(HC):
                    k = hf * HC + c
                    for b in range(B):
                        if k:
                            pe.wait_ge(c_s[b], k)
                        nc.tensor.matmul(bank(2 + b)[:, 0:DV], W2x[:, b * HC + c, :], Sx[:, b, k % 2, :],
                                         start=True, stop=True).then_inc(c_x[b], 1)
                    keep_clock(3, 6 if c < 8 else 0)
                    for b in range(B):
                        n = b * HC + c
                        pe.wait_ge(c_u[b], k + 1)
                        nc.tensor.matmul(bank(4 + b)[:, 0:DV], KDx[:, n, :], Wd[:, n, 0:DV],
                                         start=True, stop=True).then_inc(c_sp[b], 1)
                        o = bank((6 if c < 8 else 0) + b)[:, c % 8 * DV:(c % 8 + 1) * DV]
                        nc.tensor.matmul(o, QGx[:, n, :], Sx[:, b, k % 2, :], start=True, stop=False)
                        nc.tensor.matmul(o, ATx[:, n, :], Wd[:, n, 0:DV], start=False, stop=True).then_inc(c_o[b], 1)
                    if c < HC - 1:
                        keep_clock(3, 6 if c < 7 else 0)
                if hf == 0:
                    project_chunks(pe, 1)
                pe.wait_ge(c_ot, hf + 1)
                for b in range(B):
                    pe.wait_ge(c_s[b], HC * (hf + 1))
                    pe.wait_ge(c_oe, 4 * hf + 4)
                    for j, x in enumerate((OT0, OT1)):
                        mm = nc.tensor.matmul(bank(2 + b), WS[:, j, :],
                                              x[:, b * HC:(b + 1) * HC, :].rearrange("p n t -> p (n t)"),
                                              start=j == 0, stop=j == 1)
                    mm.then_inc(c_y, 1)
                for b in range(B):
                    pe.wait_ge(c_ye, 2 * hf + b + 1)
                    for j in range(4):
                        o = bank(4 + b)[:, j * P:(j + 1) * P]
                        c0 = b * S + hf * HT + j * P
                        nc.tensor.matmul(o, YT[:, b, j * P:(j + 1) * P], Wou[:, 0, :], start=True, stop=False)
                        mm = nc.tensor.matmul(o, ZS[:, c0:c0 + P], Wou[:, 1, :], start=False, stop=True)
                    mm.then_inc(c_f, 1)

        def project_chunks(pe, hf):
            if hf == 0:
                pe.wait_ge(c_xce, 8)
                keep_clock(112, 6)
            pe.wait_ge(c_wc, 1)
            for g in range(NG):
                m = hf * NG + g
                pe.wait_ge(c_xs, 1 if PJG * (g + 1) <= HC else 2)
                if m >= 2:
                    pe.wait_ge(c_pje, m - 1)
                if hf == 1 and g == 0:
                    pe.wait_ge(c_oe, 4)
                for i in range(min(PJG, NH - PJG * g)):
                    n = PJG * g + i
                    b, c = divmod(n, HC)
                    c0 = b * S + hf * HT + CH * c
                    for h in range(GH):
                        mm = nc.tensor.matmul(bank(m % 2)[band(h), i * NPJ:(i + 1) * NPJ], XS[:, c0:c0 + CH],
                                              WC[:, h, :], start=True, stop=True)
                mm.then_inc(c_pj, 1)

        def keep_clock(n, b):
            for i in range(n):
                nc.tensor.matmul(bank(b)[:, 8 * DV:512], identb[:, :], identb[:, :], start=True, stop=True)

        def c_act(act, ca):
            act.wait_ge(c_ld, C_LD)
            for q in range(4):
                if q == 0:
                    act.wait_ge(b_lg, 1)
                ln_copy(act, 2, q, (0, 1, 2, 3)[q])
            for n in range(8):
                q, w = divmod(n, 2)
                b, o = divmod(512 * q, S)
                act.wait_ge(c_xc, n + 1)
                nc.scalar.activation((XC, ZC)[w][:, b, 1 + o:1 + o + 512], bank(4 + n % 4), ACT.Copy).then_inc(c_xce, 1)
            for b in range(B):
                act.wait_ge(c_cv, b + 1)
                nc.scalar.activation(XS[:, b * S:(b + 1) * S], XS[:, b * S:(b + 1) * S], ACT.Silu).then_inc(c_xs, 1)
            for hf in range(2):
                if hf == 0:
                    copy_projections(act, 0)
                act.wait_ge(c_zz, hf + 1)
                nc.scalar.activation(sm[:, 10, :], sm[:, 1, :], ACT.Exp, scale=-1.0)
                nc.scalar.activation(sm[:, 13, 0:1], par[:, 0:1], ACT.Exp)
                ca.fence(nc.scalar.activation(sm[:, 3, :], sm[:, 3, :], ACT.Exp, scale=-1.0))
                nc.scalar.activation(sm[:, 4, :], sm[:, 3, :], ACT.Ln, bias=1.0).then_inc(c_ga, 1)
                act.wait_ge(c_ss, hf + 1)
                ca.fence(nc.scalar.activation(rs[:, :, :], ss[:, :, :], ACT.Ln))
                nc.scalar.activation(rs[:, :, :], rs[:, :, :], ACT.Exp, scale=-0.5).then_inc(c_rs, 1)
                act.wait_ge(c_kq, hf + 1)
                if hf == 0:
                    act.wait_ge(c_z, 5)
                else:
                    act.wait_ge(c_w, NR)
                for h in range(GH):
                    nc.scalar.activation(KTx[band(h), :, 32 * h:32 * h + 32], KQ[band(h), :, 0:32],
                                         ACT.Copy).then_inc(c_kx, 1)
                act.wait_ge(c_gs, hf + 1)
                nc.scalar.activation(sm[:, 5:8, :], gsum[:, :, :], ACT.Exp
                                     ).then_inc(c_ge, 1)
                act.wait_ge(c_dd, hf + 1)
                nc.scalar.activation(Ed[:, :, :], Ed[:, :, :], ACT.Exp).then_inc(c_ed, 1)
                act.wait_ge(c_pje, NG * (hf + 1))
                g0 = 2 * DK + DV
                nc.scalar.activation(PJ[:, :, g0:g0 + DV], PJ[:, :, g0:g0 + DV], ACT.Silu).then_inc(c_gg, 1)
                if hf == 0:
                    for q in range(4):
                        act.wait_ge(c_zp, q + 1)
                        nc.scalar.activation(ZS[:, 512 * q:512 * q + 512], bank(7), ACT.Silu,
                                             bias=cb[:, 1:2]).then_inc(c_zs, 1)
                for g in range(NR):
                    m = hf * NR + g
                    w = min(RG, NH - RG * g)
                    act.wait_ge(c_w, m + 1)
                    nc.scalar.activation(Wd[:, RG * g:RG * g + w, :].rearrange("p n c -> p (n c)"),
                                         bank(g % 2)[:, 0:w * RW], ACT.Copy).then_inc(c_we, 1)
                for g in range(2):
                    for b in range(B):
                        act.wait_ge(c_o[b], hf * HC + 8 * g + 8)
                        n = b * HC + 8 * g
                        nc.scalar.activation(Os[:, n:n + 8, 0:DV],
                                             bank((6 if g == 0 else 0) + b)[:, 0:8 * DV].rearrange(
                                                 "p (n v) -> p n v", v=DV), ACT.Copy).then_inc(c_oe, 1)
                act.wait_ge(c_os, hf + 1)
                ca.fence(nc.scalar.activation(sm[:, 12, :], sm[:, 11, :], ACT.Ln))
                nc.scalar.activation(sm[:, 12, :], sm[:, 12, :], ACT.Exp, scale=-0.5).then_inc(c_or, 1)
                if hf == 0:
                    copy_projections(act, 1)
                for b in range(B):
                    act.wait_ge(c_y, 2 * hf + b + 1)
                    if hf:
                        act.wait_ge(c_f, b + 1)
                    nc.scalar.activation(YT[:, b, :], bank(2 + b), ACT.Copy).then_inc(c_ye, 1)

        def copy_projections(act, hf):
            if hf:
                act.wait_ge(c_gm, 1)
            for g in range(NG):
                m = hf * NG + g
                w = min(PJG, NH - PJG * g)
                act.wait_ge(c_pj, m + 1)
                nc.scalar.activation(PJ[:, PJG * g:PJG * g + w, :].rearrange("p n c -> p (n c)"),
                                     bank(m % 2)[:, 0:w * NPJ], ACT.Copy).then_inc(c_pje, 1)

        def newton(v, y, x, w):
            v.fence(nc.vector.tensor_tensor(w, y, y, ALU.mult))
            v.fence(nc.vector.tensor_tensor(w, w, x, ALU.mult))
            v.fence(nc.vector.tensor_scalar(w, w, -0.5, 1.5, ALU.mult, ALU.add))
            v.fence(nc.vector.tensor_tensor(y, y, w, ALU.mult))

        def c_dve(dve, v):
            dve.wait_ge(c_ld, C_LD)
            nc.vector.tensor_copy(WC[:, :, NPJ - 2:NPJ], wgb[:, :, :].rearrange("p w h -> p h w")).then_inc(c_wc, 1)
            for j in range(4):
                i = nc.vector.tensor_scalar(dgw[:, j, :], ident[:, :], cw[:, 1, j:j + 1], None, ALU.mult)
            i.then_inc(c_dg, 1)
            dve.wait_ge(c_pad, 4)
            for b in range(B):
                dve.wait_ge(c_xce, 4 * b + 3)
                y = XS[:, b * S:(b + 1) * S]
                v.fence(nc.vector.tensor_scalar(y, XC[:, b, 0:S], cw[:, 0, 0:1], cb[:, 0:1], ALU.mult, ALU.add))
                for j in range(1, 4):
                    i = nc.vector.scalar_tensor_tensor(y, XC[:, b, j:j + S], cw[:, 0, j:j + 1], y, ALU.mult, ALU.add)
                    if j < 3:
                        v.fence(i)
                i.then_inc(c_cv, 1)
            for hf in range(2):
                if hf:
                    dve.wait_ge(c_or, 1)
                    dve.wait_ge(c_w, NR)
                sq = R[:, :, 0:2 * DK]
                for n, groups in ((slice(0, 6 * PJG), 6), (slice(6 * PJG, NH), NG)):
                    dve.wait_ge(c_pje, NG * hf + groups)
                    if groups == NG:
                        nc.vector.tensor_scalar(sm[:, 1, :], PJ[:, :, NPJ - 1], par[:, 2:3], None, ALU.add)
                        v.fence(nc.vector.tensor_scalar(sm[:, 0, :], PJ[:, :, NPJ - 2], par[:, 1:2], None, ALU.add))
                        nc.vector.scalar_tensor_tensor(sm[:, 3, :], sm[:, 0, :], -1.0, sm[:, 0, :], ALU.mult, ALU.max
                                                       ).then_inc(c_zz, 1)
                    v.fence(nc.vector.tensor_tensor(sq[:, n, :], PJ[:, n, 0:2 * DK], PJ[:, n, 0:2 * DK], ALU.mult))
                    i = nc.vector.tensor_reduce(ss[:, n, :], sq[:, n, :].rearrange("p n (a k) -> p n a k", k=DK),
                                                AX.X, ALU.add)
                v.fence(i)
                nc.vector.tensor_scalar(ss[:, :, :], ss[:, :, :], 1e-6, None, ALU.add).then_inc(c_ss, 1)
                dve.wait_ge(c_ga, hf + 1)
                v.fence(nc.vector.tensor_scalar(sm[:, 14, :], sm[:, 0, :], 0.0, None, ALU.max))
                v.fence(nc.vector.tensor_tensor(sm[:, 14, :], sm[:, 14, :], sm[:, 4, :], ALU.add))
                nc.vector.tensor_scalar(sm[:, 2, :], sm[:, 14, :], sm[:, 13, 0:1], -1.0, ALU.mult, ALU.mult
                                        ).then_inc(c_gk, 1)
                v.fence(nc.vector.tensor_scalar(sm[:, 15, :], sm[:, 10, :], 1.0, None, ALU.add))
                v.fence(nc.vector.reciprocal(sm[:, 8, :], sm[:, 15, :]))
                dve.wait_ge(c_rs, hf + 1)
                if hf == 0:
                    dve.wait_ge(c_clr, 3)
                newton(v, rs, ss, sm[:, 14:16, :].rearrange("p a n -> p (a n)").rearrange("p (n a) -> p n a", a=2))
                nc.vector.tensor_tensor(KN[:, :, 0:DK], PJ[:, :, DK:2 * DK], rowwise(rs[:, :, 1], DK), ALU.mult)
                v.fence(nc.vector.tensor_tensor(QN[:, :, 0:DK], PJ[:, :, 0:DK], rowwise(rs[:, :, 0], DK), ALU.mult))
                nc.vector.transpose(KQ[:, :, 0:32], KN[:, :, :]).then_inc(c_n, 1)
                nc.vector.transpose(KQ[:, :, 32:64], QN[:, :, :]).then_inc(c_kq, 1)
                dve.wait_ge(c_gc, hf + 1)
                v.fence(nc.vector.tensor_copy(gsum[:, 0:3:2, :], bank(6)[:, 0:2 * NH].rearrange("p (a n) -> p a n", a=2)))
                nc.vector.tensor_tensor(gsum[:, 1, :], gsum[:, 2, :], gsum[:, 0, :], ALU.subtract).then_inc(c_gs, 1)
                v.fence(nc.vector.transpose(Et[:, :, :], rowwise(gsum[:, 0, :], 32)))
                v.fence(nc.vector.tensor_tensor(Ed[:, :, :], rowwise(gsum[:, 0, :], 32), Et[:, :, :], ALU.subtract))
                nc.vector.tensor_tensor(Ed[:, :, :], Ed[:, :, :], dmask[:, :].unsqueeze(1).to_broadcast([P, NH, 32]),
                                        ALU.add).then_inc(c_dd, 1)
                dve.wait_ge(c_ge, hf + 1)
                nc.vector.tensor_tensor(sm[:, 9, :], sm[:, 8, :], sm[:, 5, :], ALU.mult).then_inc(c_be, 1)
                dve.wait_ge(c_ed, hf + 1)
                v.fence(nc.vector.transpose(Et[:, :, :], Ed[:, :, :]))
                v.fence(nc.vector.scalar_tensor_tensor(Ed[:, :, :], Ed[:, :, :], -1.0, rowwise(sm[:, 8, :], 32),
                                                       ALU.mult, ALU.mult))
                dve.wait_ge(c_qg, hf + 1)
                for h in range(GH):
                    i = nc.vector.transpose(QGx[band(h), :, 32 * h:32 * h + 32], QN[band(h), :, :])
                i.then_inc(c_qx, 1)
                gram = ps[:, 2:6, :].rearrange("p b (n c) -> p (b n) c", c=64)
                for g in range(4):
                    dve.wait_ge(c_gr, 4 * hf + g + 1)
                    n = slice(8 * g, 8 * g + 8)
                    i = nc.vector.tensor_tensor(Lc[:, n, :], gram[:, n, 0:32], Ed[:, n, :], ALU.mult)
                v.fence(i)
                v.fence(nc.vector.transpose(Lp[:, :, :], Lc[:, :, :].rearrange("p n s -> p s n")))
                dve.wait_ge(c_mi, hf + 1)
                for s in range(CH - 1):
                    r, w = CH - 1 - s, s + 1
                    m = mt[:, 0:r * w].rearrange("p (t j) -> p t j", j=w)
                    v.fence(nc.vector.tensor_tensor(m, Lp[:, s, s + 1:CH].unsqueeze(2).to_broadcast([P, r, w]),
                                                    Mp[:, s, 0:w].unsqueeze(1).to_broadcast([P, r, w]), ALU.mult))
                    i = nc.vector.tensor_tensor(Mp[:, s + 1:CH, 0:w], Mp[:, s + 1:CH, 0:w], m, ALU.add)
                    if s == CH - 5:
                        i.then_inc(c_fs, 1)
                        dve.wait_ge(c_fs, hf + 1)
                    else:
                        v.fence(i)
                for h in range(GH):
                    i = nc.vector.transpose(KTx[band(h), :, 32 * h:32 * h + 32].rearrange("p n t -> p t n"),
                                            Mp[band(h), :, :])
                i.then_inc(c_tt, 1)
                for h in range(GH):
                    i = nc.vector.tensor_tensor(ATx[band(h), :, 32 * h:32 * h + 32], gram[band(h), :, 32:64],
                                                Et[band(h), :, :], ALU.mult)
                i.then_inc(c_at, 1)
                for n, groups in ((slice(0, 3 * RG), 3), (slice(3 * RG, NH), NR)):
                    dve.wait_ge(c_we, NR * hf + groups)
                    for h in range(GH):
                        i = nc.vector.transpose(W2x[band(h), n, 32 * h:32 * h + 32], Wd[band(h), n, DV:RW])
                i.then_inc(c_w2, 1)
                for c in range(HC):
                    k = hf * HC + c
                    for b in range(B):
                        n = b * HC + c
                        dve.wait_ge(c_x[b], k + 1)
                        nc.vector.tensor_tensor(Wd[:, n, 0:DV], Wd[:, n, 0:DV], bank(2 + b)[:, 0:DV],
                                                ALU.subtract).then_inc(c_u[b], 1)
                    for b in range(B):
                        n = b * HC + c
                        dve.wait_ge(c_sp[b], k + 1)
                        if k >= 1:
                            dve.wait_ge(c_o[b], k)
                            dve.wait_ge(c_s[b], k)
                        nc.vector.scalar_tensor_tensor(Sx[:, b, (k + 1) % 2, :], Sx[:, b, k % 2, :],
                                                       sm[:, 7, n:n + 1],
                                                       bank(4 + b)[:, 0:DV], ALU.mult, ALU.add).then_inc(c_s[b], 1)
                dve.wait_ge(c_oe, 4 * hf + 4)
                o2 = R[:, :, 0:DV]
                v.fence(nc.vector.tensor_tensor(o2, Os[:, :, 0:DV], Os[:, :, 0:DV], ALU.mult))
                v.fence(nc.vector.tensor_reduce(sm[:, 11, :], o2, AX.X, ALU.add))
                nc.vector.tensor_scalar(sm[:, 11, :], sm[:, 11, :], 1.0 / DV, EPS, ALU.mult, ALU.add).then_inc(c_os, 1)
                dve.wait_ge(c_gw, hf + 1)
                g0 = 2 * DK + DV
                nc.vector.tensor_tensor(Os[:, :, 0:DV], Os[:, :, 0:DV], PJ[:, :, g0:g0 + DV], ALU.mult).then_inc(c_gm, 1)
                dve.wait_ge(c_gm, hf + 1)
                dve.wait_ge(c_or, hf + 1)
                newton(v, sm[:, 12, :], sm[:, 11, :], sm[:, 14, :])
                v.fence(nc.vector.tensor_tensor(Os[:, :, 0:DV], Os[:, :, 0:DV], rowwise(sm[:, 12, :], DV), ALU.mult))
                v.fence(nc.vector.transpose(OT0[:, :, :], Os[:, :, 0:32]))
                nc.vector.transpose(OT1[:, :, :], Os[:, :, 32:64]).then_inc(c_ot, 1)
                for b in range(B):
                    dve.wait_ge(c_f, 2 * hf + b + 1)
                    k0 = b * BPB + hf * 4
                    x = X[:, k0:k0 + 4, :].rearrange("p k d -> p (k d)")
                    nc.vector.tensor_tensor(x, bank(4 + b), x, ALU.add).then_inc(c_fx, 1)

        cctx.close()

        WT = sb("WT", [P, 3, D], F32)
        XP = sb("XP", [P, B, 1 + S], F32)
        XPW = sb("XPW", [P, 2, 2, 512], F32)
        XM = sb("XM", [P, 2, NT], F32)
        KA = sb("KA", [P, NT], F32)
        SG = sb("SG", [P, NB, D], F32)

        d_cst = sem("d_cst")
        d_wt = sem("d_wt")
        d_wc = sem("d_wc")
        d_sh = sem("d_sh")
        d_mx = sem("d_mx")
        d_r = sem("d_r")
        d_sg = sem("d_sg")
        d_k = sem("d_k")
        d_ka = sem("d_ka")
        d_v = sem("d_v")
        d_g = sem("d_g")
        d_x = sem("d_x")

        def d_sync(sp):
            for q in range(4):
                sp.wait_ge(d_x, q + 1)
                sp.dma_start(out_tok[:, 4 * q:4 * q + 4, :], X[:, 4 * q:4 * q + 4, :]).then_inc(s_out, 16)
            sp.wait_ge(s_out, 64)

        def d_pool(pool):
            pool.wait_ge(c_fx, 4)
            nc.gpsimd.memset(XP[:, :, 0:1], 0.0).then_inc(d_cst, 1)
            for q in range(4):
                ln_power(pool, 3, q)

        def d_pe(pe):
            pe.wait_ge(c_fx, 4)
            pe.wait_ge(d_ld, 80)
            for i in range(3):
                mm = nc.tensor.transpose(bank(4)[:, i * P:(i + 1) * P], Wn[:, i, :], ident[:, :])
            mm.then_inc(d_wt, 1)
            for q in range(4):
                ln_transpose(pe, 3, q, q)
            pe.wait_ge(d_wc, 1)
            for q in range(5):
                if q < 4:
                    cols = slice(512 * q, 512 * q + 512)
                    pe.wait_ge(d_mx, 2 * q + 1)
                    for j in range(4):
                        c0 = 512 * q + j * P
                        mm = nc.tensor.matmul(bank(q)[:, j * P:(j + 1) * P], XM[:, 0, c0:c0 + P], WT[:, 0, :],
                                              start=True, stop=True)
                    mm.then_inc(d_r, 1)
                    pe.wait_ge(d_mx, 2 * q + 2)
                    if q >= 2:
                        pe.wait_ge(d_ka, q - 1)
                    nc.tensor.matmul(bank(4 + q % 2), WT[:, 1, :], XM[:, 1, cols], start=True, stop=True).then_inc(d_k, 1)
                if q >= 1:
                    pe.wait_ge(d_ka, q)
                    if q >= 3:
                        pe.wait_ge(d_g, q - 2)
                    for j in range(4):
                        c0 = 512 * (q - 1) + j * P
                        mm = nc.tensor.matmul(bank(6 + (q - 1) % 2)[:, j * P:(j + 1) * P], KA[:, c0:c0 + P],
                                              WT[:, 2, :], start=True, stop=True)
                    mm.then_inc(d_v, 1)

        def d_act(act):
            act.wait_ge(d_wt, 1)
            nc.scalar.activation(WT[:, :, :].rearrange("p i d -> p (i d)"), bank(4)[:, 0:3 * P],
                                 ACT.Copy).then_inc(d_wc, 1)
            for q in range(5):
                if q < 4:
                    b, o = divmod(512 * q, S)
                    act.wait_ge(ln_tr, 12 + q + 1)
                    nc.scalar.activation(XP[:, b, 1 + o:1 + o + 512], bank(q), ACT.Copy).then_inc(ln_xt, 1)
                    act.wait_ge(ln_xt, 12 + q + 1)
                    act.wait_ge(d_cst, 2)
                    if q >= 2:
                        act.wait_ge(d_mx, 2 * q - 2)
                    for w in range(2):
                        nc.scalar.activation(XPW[:, w, q % 2, :], XP[:, b, o:o + 512], ACT.Copy,
                                             scale=om[:, w:w + 1]).then_inc(d_sh, 1)
                if q >= 1:
                    act.wait_ge(d_r, q)
                    nc.scalar.activation(SG[:, 4 * q - 4:4 * q, :].rearrange("p k d -> p (k d)"), bank(q - 1),
                                         ACT.Sigmoid).then_inc(d_sg, 1)

        def d_dve(dve, v):
            dve.wait_ge(c_fx, 4)
            dve.wait_ge(d_ld, 80)
            nc.vector.tensor_scalar(om[:, :], mu[:, :], -1.0, 1.0, ALU.mult, ALU.add).then_inc(d_cst, 1)
            for q in range(4):
                ln_stats(v, q)
            for q in range(4):
                ln_apply(dve, 3, q)
            for q in range(6):
                if q < 4:
                    b, o = divmod(512 * q, S)
                    for w in range(2):
                        dve.wait_ge(d_sh, 2 * q + w + 1)
                        nc.vector.scalar_tensor_tensor(XM[:, w, 512 * q:512 * q + 512], XP[:, b, 1 + o:1 + o + 512],
                                                       mu[:, w:w + 1], XPW[:, w, q % 2, :],
                                                       ALU.mult, ALU.add).then_inc(d_mx, 1)
                if 1 <= q <= 4:
                    dve.wait_ge(d_k, q)
                    k = KA[:, 512 * (q - 1):512 * q]
                    v.fence(nc.vector.tensor_scalar(k, bank(4 + (q - 1) % 2), 0.0, None, ALU.max))
                    nc.vector.tensor_tensor(k, k, k, ALU.mult).then_inc(d_ka, 1)
                if q >= 2:
                    n = q - 2
                    g = SG[:, 4 * n:4 * n + 4, :].rearrange("p k d -> p (k d)")
                    x = X[:, 4 * n:4 * n + 4, :].rearrange("p k d -> p (k d)")
                    dve.wait_ge(d_v, n + 1)
                    dve.wait_ge(d_sg, n + 1)
                    nc.vector.tensor_tensor(g, bank(6 + n % 2), g, ALU.mult).then_inc(d_g, 1)
                    dve.wait_ge(d_g, n + 1)
                    nc.vector.tensor_tensor(x, x, g, ALU.add).then_inc(d_x, 1)

        block = ctx.enter_context(nc.Block())

        @block.sync
        def _(sp):
            loads(sp)
            a_sync(sp)
            b_sync(sp)
            d_sync(sp)

        @block.gpsimd
        def _(pool):
            c = Count(pool, s_pool)
            a_pool(pool, c)
            b_pool(pool, c)
            c_pool(pool, c)
            d_pool(pool)

        @block.scalar
        def _(act):
            a_act(act)
            b_act(act)
            c_act(act, Count(act, s_act))
            d_act(act)

        @block.tensor
        def _(pe):
            a_pe(pe)
            b_pe(pe)
            c_pe(pe)
            d_pe(pe)

        @block.vector
        def _(dve):
            v = Count(dve, s_dve)
            a_dve(dve, v)
            b_dve(dve, v)
            c_dve(dve, v)
            d_dve(dve, v)


def kernel(**inputs):
    import numpy as _np
    import concourse.bacc as _bacc
    from concourse import mybir as _mybir
    from concourse.bass_utils import run_bass_kernel_spmd as _run

    nc = _bacc.Bacc("TRN2", target_bir_lowering=False, num_devices=1)
    arrays, tensors = {}, {}
    for name in inputs:
        a = _np.ascontiguousarray(inputs[name])
        arrays[f"in_{name}_dram"] = a
        tensors[name] = nc.dram_tensor(f"in_{name}_dram", a.shape, _mybir.dt.from_np(a.dtype),
                                       kind="ExternalInput").ap()
    tensors["out"] = nc.dram_tensor("out_0_dram", (B, S, D), _mybir.dt.float32, kind="ExternalOutput").ap()
    program(nc, tensors)
    r = _run(nc, [arrays], core_ids=[0])
    return r.results[0]["out_0_dram"]
```
